# Optimizing a Trainium2 kernel written in Bass

```python
import numpy as np
import jax
import jax.numpy as jnp

def _softmax(x, axis=-1):
    return jax.nn.softmax(x, axis=axis)

def _gelu(x):
    return jax.nn.gelu(x, approximate=True)

def _silu(x):
    return jax.nn.silu(x)

def _sigmoid(x):
    return jax.nn.sigmoid(x)

def _layernorm(x, axis=-1, eps=1e-05):
    m = jnp.mean(x, axis=axis, keepdims=True)
    v = jnp.var(x, axis=axis, keepdims=True)
    return (x - m) / jnp.sqrt(v + eps)

def _scatter_add(tgt, idx, src, axis=0):
    return tgt.at[idx].add(src)

def _segment_sum(src, seg, n):
    return jax.ops.segment_sum(src, seg, n)
kernel_name = 'mk_sandwich_d1_jaxref_r4_703b8e'

def setup_inputs(seed: int=0):
    np.random.seed(seed)
    _w = jnp.asarray

    def _L0_attn_setup():
        import jax, jax.numpy as jnp
        import numpy as np
        B, L, D_MODEL, D_STATE = (8, 1024, 256, 64)
        key = jax.random.key(seed)
        k1, k2, k3, k4 = jax.random.split(key, 4)
        u = jax.random.normal(k1, (B, L, D_MODEL), dtype=jnp.float32)
        A_log = jnp.log(jnp.arange(1, D_STATE + 1, dtype=jnp.float32))
        D = jax.random.normal(k2, (D_MODEL,), dtype=jnp.float32)
        C_re = jax.random.normal(k3, (D_MODEL, D_STATE), dtype=jnp.float32)
        C_im = jax.random.normal(k4, (D_MODEL, D_STATE), dtype=jnp.float32)
        log_dt = jnp.log(jnp.full((D_MODEL,), 0.01, dtype=jnp.float32))
        return {'u': u, 'A_log': A_log, 'D': D, 'C_re': C_re, 'C_im': C_im, 'log_dt': log_dt}
    _L0_attn_in = _L0_attn_setup()

    def _L0_ffn_setup():
        import jax, jax.numpy as jnp
        import numpy as np
        E = 8
        K = 2
        DIM = 256
        DFF = 512

        def _moe(x, Wg, bg, w1, w2):
            B, S, D = x.shape
            t = x.reshape(-1, D)
            logits = t @ Wg.T + bg
            probs = jax.nn.softmax(logits, axis=-1)
            topw, topi = jax.lax.top_k(probs, K)
            topw = topw / jnp.sum(topw, axis=-1, keepdims=True)
            combine = jnp.sum(jax.nn.one_hot(topi, E, dtype=t.dtype) * topw[..., None], axis=1)

            def body(acc, packed):
                w1e, w2e, ce = packed
                h = t @ w1e.T
                gate, up = jnp.split(h, 2, axis=-1)
                a = jax.nn.silu(gate) * up
                o = a @ w2e.T
                return (acc + ce[:, None] * o, None)
            out, _ = jax.lax.scan(body, jnp.zeros_like(t), (w1, w2, combine.T))
            return out.reshape(B, S, D)
        key = jax.random.key(seed)
        ks = jax.random.split(key, 5)
        B, S = (4, 512)
        x = jax.random.normal(ks[0], (B, S, DIM), dtype=jnp.float32)
        Wg = jax.random.normal(ks[1], (E, DIM), dtype=jnp.float32) * 0.02
        bg = jax.random.normal(ks[2], (E,), dtype=jnp.float32) * 0.02
        w1 = jax.random.normal(ks[3], (E, DFF, DIM), dtype=jnp.float32) * 0.02
        w2 = jax.random.normal(ks[4], (E, DIM, DFF // 2), dtype=jnp.float32) * 0.02
        return {'x': x, 'Wg': Wg, 'bg': bg, 'w1': w1, 'w2': w2}
    _L0_ffn_in = _L0_ffn_setup()
    _d = {'L0_attn_u': _L0_attn_in['u'], 'L0_attn_A_log': _L0_attn_in['A_log'], 'L0_attn_D': _L0_attn_in['D'], 'L0_attn_C_re': _L0_attn_in['C_re'], 'L0_attn_C_im': _L0_attn_in['C_im'], 'L0_attn_log_dt': _L0_attn_in['log_dt'], 'L0_ffn_Wg': _L0_ffn_in['Wg'], 'L0_ffn_bg': _L0_ffn_in['bg'], 'L0_ffn_w1': _L0_ffn_in['w1'], 'L0_ffn_w2': _L0_ffn_in['w2']}
    _x0 = _d['L0_attn_u']
    _d['L0_attn_u'] = jax.random.normal(jax.random.fold_in(jax.random.key(seed), 1), (8, 2048, 256), dtype=_x0.dtype)
    del _x0
    return _d

def reference(L0_attn_u, L0_attn_A_log, L0_attn_D, L0_attn_C_re, L0_attn_C_im, L0_attn_log_dt, L0_ffn_Wg, L0_ffn_bg, L0_ffn_w1, L0_ffn_w2):

    def _L0_attn_ref(u, A_log, D, C_re, C_im, log_dt):
        import jax, jax.numpy as jnp
        import numpy as np
        B, L, D_MODEL, D_STATE = (8, 1024, 256, 64)
        L_ = u.shape[1]
        dt = jnp.exp(log_dt)
        A = -jnp.exp(A_log)
        t = jnp.arange(L_, dtype=u.dtype)
        at = dt[:, None, None] * A[None, None, :] * t[None, :, None]
        K = jnp.einsum('mn,mln->ml', C_re, jnp.exp(at))
        u_f = jnp.fft.rfft(u.transpose(0, 2, 1), n=2 * L_)
        k_f = jnp.fft.rfft(K, n=2 * L_)
        y = jnp.fft.irfft(u_f * k_f, n=2 * L_)[..., :L_]
        return y.transpose(0, 2, 1) + u * D

    def _L0_ffn_ref(x, Wg, bg, w1, w2):
        import jax, jax.numpy as jnp
        import numpy as np
        E = 8
        K = 2
        DIM = 256
        DFF = 512

        def _moe(x, Wg, bg, w1, w2):
            B, S, D = x.shape
            t = x.reshape(-1, D)
            logits = t @ Wg.T + bg
            probs = jax.nn.softmax(logits, axis=-1)
            topw, topi = jax.lax.top_k(probs, K)
            topw = topw / jnp.sum(topw, axis=-1, keepdims=True)
            combine = jnp.sum(jax.nn.one_hot(topi, E, dtype=t.dtype) * topw[..., None], axis=1)

            def body(acc, packed):
                w1e, w2e, ce = packed
                h = t @ w1e.T
                gate, up = jnp.split(h, 2, axis=-1)
                a = jax.nn.silu(gate) * up
                o = a @ w2e.T
                return (acc + ce[:, None] * o, None)
            out, _ = jax.lax.scan(body, jnp.zeros_like(t), (w1, w2, combine.T))
            return out.reshape(B, S, D)
        return _moe(x, Wg, bg, w1, w2)
    x = L0_attn_u
    x = x + _layernorm(_L0_attn_ref(_layernorm(x, axis=-1), L0_attn_A_log, L0_attn_D, L0_attn_C_re, L0_attn_C_im, L0_attn_log_dt), axis=-1)
    x = x + _layernorm(_L0_ffn_ref(_layernorm(x, axis=-1), L0_ffn_Wg, L0_ffn_bg, L0_ffn_w1, L0_ffn_w2), axis=-1)
    return x

_drawn_inputs = setup_inputs


def setup_inputs(seed=0):
    import zlib

    import numpy as np

    out = dict(_drawn_inputs(seed))
    spreads = {'L0_attn_log_dt': (-4.605170249938965, 0.2)}
    factors = {}
    for name, (base, spread) in spreads.items():
        noise = np.random.default_rng([zlib.crc32(name.encode()), seed]).standard_normal(out[name].shape)
        drawn = base * np.exp(spread * noise) if base else spread * noise
        out[name] = jnp.asarray(drawn.astype(out[name].dtype))
    for name, factor in factors.items():
        out[name] = (out[name] * factor).astype(out[name].dtype)
    return out
```

```python
from contextlib import ExitStack

import numpy as np
import concourse.bass as bass
from concourse import mybir

F32 = mybir.dt.float32
I32 = mybir.dt.int32
ALU = mybir.AluOpType
ACT = mybir.ActivationFunctionType
AX = mybir.AxisListType

P = 128
B, L, C = 8, 2048, 256
NS = 64
E, K2 = 8, 2
DFF = 512
HF = DFF // 2
CH = L // P
NT = B * CH
KC = C // P
GB = 4
NG = NT // GB
PARTS = 4
GP = NG // PARTS
TP = NT // PARTS
CAPT = TP + 1
CAPR = CAPT * P
MT = TP * K2 + E
MP = MT // 2
SG = 8
NSG = C // SG
PR = SG // 2
NQ = 8
EPS = 1e-5


class Steps:

    def __init__(self, engine, sem, per, at):
        self.engine, self.sem, self.per, self.at, self.done = engine, sem, per, at, 0

    def __call__(self, instruction):
        instruction.then_inc(self.sem, 1)
        self.done += 1

    def wait(self):
        self.engine.wait_ge(self.sem, self.at * self.per + self.done)

    def end(self):
        assert self.done == self.per, (self.done, self.per)


def ssm_moe_block(nc, u, A_log, D, C_re, log_dt, Wg, bg, w1, w2, out):
    ctx = ExitStack()
    with ctx:
        def sem(name):
            return ctx.enter_context(nc.semaphore(name))

        def sems(name, n=2):
            return [sem(f"{name}{i}") for i in range(n)]

        def region(name, words, dt=F32):
            return ctx.enter_context(nc.sbuf_tensor(name, [P, words], dt))

        class Carve:

            def __init__(self, base, size):
                self.base, self.size, self.at = base, size, 0

            def take(self, *shape):
                n = int(np.prod(shape))
                v = self.base[:, self.at:self.at + n]
                self.at += n
                assert self.at <= self.size, (self.at, self.size)
                names = " ".join(f"d{i}" for i in range(len(shape)))
                if len(shape) == 1:
                    return v
                return v.rearrange(f"p ({names}) -> p {names}", **{f"d{i}": s for i, s in enumerate(shape)})

            def two(self, *shape):
                return [self.take(*shape), self.take(*shape)]

        def scratch(name, shape):
            return nc.dram_tensor(name, shape, F32, kind="Internal").ap()

        toep_dram = scratch("toeplitz", (C, P, P))
        w1_dram = scratch("w1_transposed", (P, KC, E, DFF))
        w2_dram = scratch("w2_transposed", (P, KC, E, C))
        x2_dram = scratch("x_after_ssm", (NT * P, C))
        list_dram = [scratch(f"expert_rows{p}", (E * CAPR, C)) for p in range(PARTS)]
        eo_dram = [scratch(f"expert_out{p}", (MT * P, C)) for p in range(PARTS)]
        u_rows = u.rearrange("b (a p) c -> p (b a) c", p=P)
        x2_rows = x2_dram.rearrange("(t p) c -> p t c", p=P)
        out_rows = out.rearrange("b (a p) c -> p (b a) c", p=P)

        PSZ = C * TP
        hid = region("hid", PARTS * PSZ)
        H = hid[:, :].rearrange("p (q c t) -> p q c t", q=PARTS, c=C)
        wide_size = E * KC * (DFF + C)
        wide = region("wide", wide_size)
        group = region("group", 4 * GB * C)
        slots = group[:, :].rearrange("p (s t c) -> p s t c", s=4, t=GB)
        small = Carve(region("small", 3500), 3500)
        ident = small.take(P)
        before = small.take(P)
        ones = small.take(P)
        minus_half = small.take(GB)
        e_base = small.take(GB)
        part_no = small.take(1)
        rev_e = small.take(E)
        cap_base = small.take(E)
        scan_keep = small.take(E * GB)
        zero_row = small.take(C)
        wgT = small.take(KC, E)
        bg_row = small.take(E)
        tTs = small.two(KC, P)
        tile_no = small.take(MT)
        steps_k = small.take(TP)
        stats = [small.two(GB, 6) for _ in range(2)]
        mv = [small.two(GB, 2) for _ in range(2)]
        norm4 = [[small.take(GB) for _ in range(4)] for _ in range(4)]
        norm8 = [[small.take(GB) for _ in range(4)] for _ in range(2)]
        lg, lg2, tmp, tmp2, oh1, oh2, pos = [small.two(GB, E) for _ in range(7)]
        best, best2, pick, gap, eg, wsum = [small.two(GB) for _ in range(6)]
        chosen, seen = [small.two(E * GB) for _ in range(2)]
        rank_base = small.two(E)
        run = small.take(E)
        w_tab = small.take(K2, NT)
        slot_tab = small.take(K2, NT)
        small_i = Carve(region("small_i", 320, I32), 320)
        slot_tab_i = small_i.take(K2, NT)
        idx = small_i.two(K2, GB)
        idx_f = small_i.two(K2, GB)
        idx_pad = small_i.take(E)
        mb = Carve(hid[:, 0:PSZ], PSZ)
        xin = mb.two(2, C)
        xT = mb.two(2, KC, P)
        gate = mb.two(2, HF)
        act_b = mb.two(2, HF)
        aT = mb.two(2, KC, P)
        o_b = mb.two(2, C)
        tabs_i = Carve(mb.take(2 * PARTS * MT).bitcast(I32), 2 * PARTS * MT)
        in_tile = tabs_i.take(PARTS, MT)
        tile_e = tabs_i.take(PARTS, MT)
        tabs = mb
        over = tabs.take(E, TP)
        counts, ntile, ends, starts, delta, step_d = [tabs.take(E) for _ in range(6)]
        last_t = tabs.take(1)
        t_at, e_of, st_of = [tabs.take(MT) for _ in range(3)]
        g_e = tabs.take(MT, E - 1)
        shift = over.rearrange("p e t -> p (e t)")[:, 0:K2 * TP].rearrange("p (k t) -> p k t", k=K2)

        wb = Carve(wide, wide_size)
        toep = wb.two(SG, P)
        vrow = wb.two(PR, 2, NS)
        arg = wb.two(PR, P + 1)
        e1 = wb.two(PR, 3 * NS)
        e2 = wb.two(PR, P + 1)
        wb_e2c = wb.at
        e2c = wb.two(PR, P)
        decay = wb.two(PR * NT)
        wb_state = wb.at
        state = wb.two(PR, NT)
        iota_l = wb.take(P + 1)
        decay_mask = wb.take(NT)
        rev_pos = wb.take(1)
        dt_row = wb.take(C)
        a_row = wb.take(NS)
        a_col = wb.take(1)
        wd = wb.take(C // 2)
        ct = wb.take(C // 2)
        d_col = wb.take(C // P)
        W1v = Carve(wide, wide_size)
        W1 = W1v.take(KC, E, DFF)
        W2 = W1v.take(KC, E, C)
        fb = Carve(hid[:, PSZ:2 * PSZ], PSZ)
        fx = fb.two(GB, C)
        gat = fb.two(K2, GB, C)
        pro = Carve(wide, 2 * SG * P)
        wrow1 = pro.take(DFF // P, C)
        wst1 = pro.take(KC, DFF)
        pro = Carve(wide[:, wb_e2c:], 2 * PR * P)
        wrow2 = pro.take(C // P, C)
        wst2 = pro.take(KC, C)
        pro = Carve(wide[:, wb_state:], 2 * PR * NT)
        cz = pro.take(C // 2, 2)
        c_rows = pro.take(P)
        wg_rows = pro.take(C)
        k_rows = slots[:, 2, 0, :]
        k_pad = slots[:, 3, 0:C // P, :]

        banks = ctx.enter_context(nc.psum_tensor("banks", [P, 8 * 512], F32))

        def bank(i, n=1):
            return banks[:, 512 * i:512 * (i + n)]

        xp = [bank(i).rearrange("p (q t) -> p q t", q=PR) for i in range(2)]
        yp = [bank(2 + 2 * i, 2).rearrange("p (m q t) -> p m q t", m=2, q=PR) for i in range(2)]
        kt_p = bank(6)[:, 0:C]
        ct_p = bank(7)[:, 0:P]
        wg_p = bank(7)[:, P:P + KC * E].rearrange("p (k e) -> p k e", k=KC)
        kr_p = bank(7)[:, 0:C].rearrange("p (h l) -> p h l", h=C // P)
        wp1 = bank(0, 2).rearrange("p (k n) -> p k n", k=KC)
        wp2 = bank(2).rearrange("p (k n) -> p k n", k=KC)
        ph = [bank(2 * i, 2).rearrange("p (t n) -> p t n", t=2) for i in range(2)]
        px = bank(4).rearrange("p (t k n) -> p t k n", t=2, k=KC)
        pa = bank(5).rearrange("p (t k n) -> p t k n", t=2, k=KC)
        po = bank(6).rearrange("p (t n) -> p t n", t=2)
        tp = [bank(6 + i)[:, 0:C].rearrange("p (k n) -> p k n", k=KC) for i in range(2)]
        lp = [bank(i)[:, 0:GB * E].rearrange("p (t e) -> p t e", t=GB) for i in range(2)]
        rp = [bank(2 + i)[:, 0:2 * E] for i in range(2)]

        passed = sem("passed")
        const_in, const_ready, exp_ready, table_ready, ct_psum = (
            sem("const_in"), sem("const_ready"), sem("exp_ready"), sem("table_ready"), sem("ct_psum"))
        a_loaded, a_dve, a_scale, a_done = sems("a_loaded", 4), sems("a_dve", 4), sems("a_scale", 4), sems("a_done", 4)
        k_arg, k_exp, k_mm = sems("k_arg"), sems("k_exp"), sems("k_mm")
        k_row, k_tr, k_ready, t_stored = sem("k_row"), sem("k_tr"), sem("k_ready"), sems("t_stored", NQ)
        w_loaded, w_psum, w_copied, w_stored = sem("w_loaded"), sem("w_psum"), sem("w_copied"), sem("w_stored")
        s_toep, s_arg, s_exp, s_coef = sems("s_toep"), sems("s_arg"), sems("s_exp"), sems("s_coef")
        s_in, s_state, s_out, s_copied = sems("s_in"), sems("s_state"), sems("s_out"), sems("s_copied")
        weights_in = sem("weights_in")
        b_x, b_saved, b_dve, b_scale, b_y = sems("b_x"), sems("b_saved"), sems("b_dve"), sems("b_scale"), sems("b_y")
        b_tp, b_tT, b_lt, b_rank, b_sent = sems("b_tp"), sems("b_tT"), sems("b_lt"), sems("b_rank"), sems("b_sent")
        q_dve, q_padded = sem("q_dve"), sem("q_padded")
        m_in, m_xp, m_xT, m_h, m_gate, m_a = (
            sems("m_in"), sems("m_xp"), sems("m_xT"), sems("m_h"), sems("m_gate"), sems("m_a"))
        m_ap, m_aT, m_o, m_oc, m_out = sems("m_ap"), sems("m_aT"), sems("m_o"), sems("m_oc"), sems("m_out")
        f_x, f_idx, f_got, f_dve, f_scale, f_z, f_saved = (
            sems("f_x"), sems("f_idx"), sems("f_got"), sems("f_dve"), sems("f_scale"), sems("f_z"), sems("f_saved"))

        def apart(engine):
            engine.sem_inc(passed, 1)

        CONSTS = 24
        TABLES = 6
        A_DVE = 10
        B_DVE = 52
        Q_DVE = 22
        F_DVE = 19
        B_VAR1, B_SUM, B_VAR2, B_ROWS, B_GAP, B_SEEN, B_IDX = 10, 11, 21, 25, 34, 40, 49
        B_EXP = 5
        GU = GP // 2
        MU = MP // 2
        SENT = 16 * K2 * GB
        block = ctx.enter_context(nc.Block())

        @block.sync
        def _(sp):
            sp.dma_start(a_col[0:NS, :], A_log.rearrange("(n o) -> n o", o=1)).then_inc(const_in, 16)
            sp.dma_start(a_col[NS:2 * NS, :], A_log.rearrange("(n o) -> n o", o=1)).then_inc(const_in, 16)
            sp.dma_start(a_row, A_log.partition_broadcast(P)).then_inc(const_in, 16)
            sp.dma_start(dt_row, log_dt.partition_broadcast(P)).then_inc(const_in, 16)
            sp.dma_start(c_rows, C_re.rearrange("(p m) n -> p (m n)", m=2)).then_inc(const_in, 16)
            for h in range(C // P):
                sp.dma_start(d_col[:, h:h + 1], D[P * h:P * h + P].rearrange("(p o) -> p o", o=1)).then_inc(const_in, 16)
            sp.dma_start(wg_rows[0:E, :], Wg).then_inc(const_in, 16)
            sp.dma_start(bg_row, bg.partition_broadcast(P)).then_inc(const_in, 16)

            with sp.Fori(0, NG // 4) as n:
                for s in range(4):
                    sp.wait_ge(a_done[s], n)
                    sp.dma_start(slots[:, s], u_rows[:, bass.ds(4 * GB * n + GB * s, GB), :]).then_inc(a_loaded[s], 16)
                sp.wait_ge(w_psum, n)
                sp.dma_start(wrow1, w1.rearrange("e (j p) k -> p e j k", p=P)[:, bass.ds(n, 1)].rearrange("p o j k -> p (o j) k")).then_inc(w_loaded, 16)
                sp.dma_start(wrow2, w2.rearrange("e (j p) k -> p e j k", p=P)[:, bass.ds(n, 1)].rearrange("p o j k -> p (o j) k")).then_inc(w_loaded, 16)
            sp.wait_ge(k_ready, 5)
            for q in range(NQ):
                h, rows = q // (NQ // 2), slice(C // NQ * (q % (NQ // 2)), C // NQ * (q % (NQ // 2)) + C // NQ)
                v = k_pad[rows, h, P - 1:2 * P - 1]
                skew = bass.AP(v.tensor, v.offset, [v.ap[0], [-1, P], [1, P]])
                sp.dma_start(toep_dram[C // NQ * q:C // NQ * q + C // NQ], skew).then_inc(t_stored[q], 16)
            sp.wait_ge(w_stored, 32 * E)
            for g in range(NSG):
                sp.wait_ge(t_stored[SG * g * NQ // C], 16)
                if g >= 2:
                    sp.wait_ge(s_out[g % 2], g // 2)
                sp.dma_start(toep[g % 2], toep_dram[SG * g:SG * g + SG].rearrange("c j i -> j c i")).then_inc(s_toep[g % 2], 16)
            for s in range(2):
                sp.wait_ge(s_copied[s], NSG // 2)
            sp.dma_start(W1, w1_dram).then_inc(weights_in, 16)
            sp.dma_start(W2, w2_dram).then_inc(weights_in, 16)

            for s in range(2):
                sp.wait_ge(a_done[s], NG // 4)
                sp.dma_start(slots[:, s], u_rows[:, GB * s:GB * s + GB, :]).then_inc(b_x[s], 16)

            def b_save(n, s):
                sp.wait_ge(b_dve[s], B_DVE * n + B_SUM)
                sp.dma_start(x2_rows[:, bass.ds(2 * GB * n + GB * s, GB), :], slots[:, s]).then_inc(b_saved[s], 16)

            with sp.Fori(0, NG // 2 - 1) as n:
                for s in range(2):
                    b_save(n, s)
                    sp.wait_ge(b_saved[s], 16 * (n + 1))
                    apart(sp)
                    sp.wait_ge(b_dve[s], B_DVE * n + B_ROWS)
                    sp.dma_start(slots[:, s], u_rows[:, bass.ds(2 * GB * n + GB * s + 2 * GB, GB), :]).then_inc(b_x[s], 16)
            for s in range(2):
                b_save(NG // 2 - 1, s)

            for p in range(PARTS):
                lists = list_dram[p].rearrange("(n r) c -> n r c", r=P)
                eouts = eo_dram[p].rearrange("(j t r) c -> r j t c", t=2, r=P)
                sp.wait_ge(q_dve, Q_DVE * (p + 1))
                sp.wait_ge(q_padded, 16 * E * (p + 1))
                for s in range(2):
                    sp.wait_ge(b_sent[s], SENT * GU * (p + 1))

                def m_load(j, n, s):
                    tiles = [sp.value_load(in_tile[0:1, p, bass.ds(2 * j + t, 1)], min_val=0, max_val=E * CAPT - 1)
                             for t in range(2)]
                    sp.wait_ge(m_xp[s], MU * p + n)
                    apart(sp)
                    for t, at in enumerate(tiles):
                        sp.dma_start(xin[s][:, t, :], lists[bass.ds(at, 1)].rearrange("o r c -> r (o c)")).then_inc(m_in[s], 16)

                def m_store(j, n, s):
                    sp.wait_ge(m_oc[s], MU * p + n + 1)
                    sp.dma_start(eouts[:, bass.ds(j, 1)].rearrange("r o t c -> r (o t) c"), o_b[s]).then_inc(m_out[s], 16)

                for s in range(2):
                    m_load(s, 0, s)
                with sp.Fori(0, MU - 1) as n:
                    for s in range(2):
                        m_load(2 * n + s + 2, n + 1, s)
                        m_store(2 * n + s, n, s)
                for s in range(2):
                    m_store(MP - 2 + s, MU - 1, s)

            for s in range(2):
                sp.wait_ge(b_saved[s], 16 * (NG // 2))
                sp.dma_start(fx[s], x2_rows[:, GB * s:GB * s + GB, :]).then_inc(f_x[s], 16)
            with sp.Fori(0, NG // 2 - 1) as n:
                for s in range(2):
                    sp.wait_ge(f_dve[s], F_DVE * (n + 1))
                    sp.dma_start(out_rows[:, bass.ds(2 * GB * n + GB * s, GB), :], fx[s]).then_inc(f_saved[s], 16)
                    sp.wait_ge(f_saved[s], 16 * (n + 1))
                    sp.dma_start(fx[s], x2_rows[:, bass.ds(2 * GB * n + GB * s + 2 * GB, GB), :]).then_inc(f_x[s], 16)
            for s in range(2):
                sp.wait_ge(f_dve[s], F_DVE * (NG // 2))
                sp.dma_start(out_rows[:, NT - 2 * GB + GB * s:NT - GB + GB * s, :], fx[s]).then_inc(f_saved[s], 16)
            for s in range(2):
                sp.wait_ge(f_saved[s], 16 * (NG // 2))

        @block.gpsimd
        def _(pool):
            st = Steps(pool, const_ready, CONSTS, 0)
            for v, x in ((ident, 0.0), (before, 1.0), (ones, 1.0), (decay_mask, 1.0), (minus_half, -0.5), (e_base, float(np.e)),
                         (scan_keep, 1.0), (zero_row, 0.0), (cz, 0.0), (e1[0], 0.0), (e1[1], 0.0)):
                st(pool.memset(v, x))
            for v, n, step, base, by in ((iota_l, P + 1, 1, 0, 0), (rev_pos, 1, 0, 1 - P, 1), (part_no, 1, 0, 0, 1), (rev_e, E, -1, E, 0),
                                         (cap_base, E, CAPR, 0, 0), (tile_no, MT, 1, 0, 0), (steps_k, TP, P, 0, 0)):
                st(pool.iota(v, [[step, n]], base=base, channel_multiplier=by, allow_small_or_imprecise_dtypes=True))
            st.wait()
            st(pool.affine_select(out=ident, in_=ident, compare_op=ALU.not_equal, fill=1.0, base=0,
                                  pattern=[[-1, P]], channel_multiplier=1))
            st(pool.affine_select(out=before, in_=before, compare_op=ALU.is_ge, fill=0.0, base=-1,
                                  pattern=[[1, P]], channel_multiplier=-1))
            st(pool.memset(decay_mask.rearrange("p (b a) -> p b a", a=CH)[:, :, 0:1], 0.0))
            st(pool.memset(scan_keep.rearrange("p (e t) -> p e t", t=GB)[:, :, 0:1], 0.0))
            st(pool.tensor_copy(run, cap_base))
            st(pool.memset(g_e, 0.0))
            st.end()

            def rstd(of, sem_, at):
                pool.tensor_tensor(of[2], of[0], minus_half, ALU.pow).then_inc(sem_, 1)
                pool.wait_ge(sem_, at + 1)
                pool.tensor_tensor(of[3], of[1], of[2], ALU.mult).then_inc(sem_, 1)

            def exponents(g, s, sem_):
                pool.tensor_tensor(arg[s], wd[:, bass.ds(PR * g, PR)].unsqueeze(2).broadcast_to([P, PR, P + 1]),
                                   iota_l.unsqueeze(1).broadcast_to([P, PR, P + 1]), ALU.mult).then_inc(sem_, 1)

            pool.wait_ge(table_ready, TABLES)
            with pool.Fori(0, NG // 4) as n:
                for s in range(4):
                    k, kn = s % 2, 2 * n + s // 2
                    pool.wait_ge(k_exp[k], kn)
                    exponents(4 * n + s, k, k_arg[k])
                    pool.wait_ge(a_dve[s], A_DVE * (n + 1))
                    rstd(norm4[s], a_scale[s], 2 * n)

            for s in range(2):
                pool.wait_ge(k_exp[s], NSG // 2)
            with pool.Fori(0, NSG // 2) as n:
                for s in range(2):
                    pool.wait_ge(s_exp[s], 2 * n)
                    pool.tensor_tensor(
                        vrow[s], dt_row[:, bass.ds(2 * SG * n + SG * s, SG)].rearrange("p (q m) -> p q m", m=2).unsqueeze(3).broadcast_to([P, PR, 2, NS]),
                        a_row.unsqueeze(1).unsqueeze(1).broadcast_to([P, PR, 2, NS]), ALU.mult).then_inc(s_arg[s], 1)
                    exponents(2 * n + s, s, s_arg[s])

            for p in range(PARTS):
                with pool.Fori(0, GU) as i:
                    n = GU * p + i
                    for s in range(2):
                        pool.wait_ge(b_dve[s], B_DVE * n + B_VAR1)
                        rstd(norm4[s], b_scale[s], B_EXP * n)
                        pool.wait_ge(b_dve[s], B_DVE * n + B_VAR2)
                        rstd(norm8[s], b_scale[s], B_EXP * n + 2)
                        pool.wait_ge(b_dve[s], B_DVE * n + B_GAP)
                        pool.tensor_tensor(eg[s], e_base, gap[s], ALU.pow).then_inc(b_scale[s], 1)
                        pool.wait_ge(b_dve[s], B_DVE * n + B_IDX)
                        apart(pool)
                        for k in range(K2):
                            for t in range(GB):
                                pool.indirect_dma_start(list_dram[p], bass.IndirectOffsetOnAxis(idx[s][:, k, t:t + 1], 0),
                                                        slots[:, 2 + s, t, :], None).then_inc(b_sent[s], 16)
                pool.wait_ge(q_dve, Q_DVE * p + 2)
                for e in range(E):
                    pool.indirect_dma_start(list_dram[p], bass.IndirectOffsetOnAxis(idx_pad[:, e:e + 1], 0),
                                            zero_row, None).then_inc(q_padded, 16)

            for s in range(2):
                pool.wait_ge(m_out[s], 16 * PARTS * MU)

            def gather(p, n, s):
                pool.wait_ge(f_got[s], SENT * n)
                pool.tensor_copy(idx_f[s], slot_tab_i[:, :, bass.ds(2 * GB * n + GB * s, GB)]).then_inc(f_idx[s], 1)
                pool.wait_ge(f_dve[s], F_DVE * n)
                pool.wait_ge(f_idx[s], n + 1)
                apart(pool)
                for k in range(K2):
                    for t in range(GB):
                        pool.indirect_dma_start(gat[s][:, k, t, :], None, eo_dram[p],
                                                bass.IndirectOffsetOnAxis(idx_f[s][:, k, t:t + 1], 0)).then_inc(f_got[s], 16)

            def f_rstd(n, s):
                pool.wait_ge(f_dve[s], F_DVE * n + F_DVE - 1)
                rstd(norm4[s], f_scale[s], 2 * n)

            for p in range(PARTS):
                gather(p, GU * p, 0)
                with pool.Fori(0, GU - 1) as i:
                    gather(p, GU * p + i, 1)
                    f_rstd(GU * p + i, 0)
                    gather(p, GU * p + i + 1, 0)
                    f_rstd(GU * p + i, 1)
                gather(p, GU * p + GU - 1, 1)
                f_rstd(GU * p + GU - 1, 0)
                f_rstd(GU * p + GU - 1, 1)

        @block.scalar
        def _(act):
            act.wait_ge(const_in, 16 * 9)
            for v in (a_col, a_row, dt_row):
                last = act.activation(v, v, ACT.Exp)
            last.then_inc(exp_ready, 1)

            act.wait_ge(const_ready, CONSTS)
            for p in range(PARTS):
                with act.Fori(0, GP // 4) as i:
                    n = GP // 4 * p + i
                    for s in range(4):
                        k, kn = s % 2, 2 * n + s // 2
                        act.wait_ge(k_arg[k], kn + 1)
                        act.wait_ge(k_mm[k], kn)
                        act.activation(e2[k], arg[k], ACT.Exp, scale=-1.0).then_inc(k_exp[k], 1)
                        act.wait_ge(a_scale[s], 2 * n + 2)
                        for t in range(GB):
                            last = act.activation(H[:, p, :, bass.ds(4 * GB * i + GB * s + t, 1)].rearrange("p c o -> p (c o)"),
                                                  slots[:, s, t, :], ACT.Identity,
                                                  scale=norm4[s][2][:, t:t + 1], bias=norm4[s][3][:, t:t + 1])
                        last.then_inc(a_done[s], 1)
                    act.wait_ge(w_copied, 2 * n + 2)
                    act.dma_start(w1_dram[:, :, bass.ds(n, 1), :].rearrange("p k o n -> p k (o n)"), wst1).then_inc(w_stored, 16)
                    act.dma_start(w2_dram[:, :, bass.ds(n, 1), :].rearrange("p k o n -> p k (o n)"), wst2).then_inc(w_stored, 16)

            for s in range(2):
                act.wait_ge(k_mm[s], NSG // 2)

            def s_powers(n, s):
                act.wait_ge(s_arg[s], 2 * n + 1)
                act.wait_ge(s_in[s], n)
                act.activation(e1[s].rearrange("p q (h n) -> p q h n", h=3)[:, :, 0:3:2, :], vrow[s], ACT.Exp,
                               scale=rev_pos).then_inc(s_exp[s], 1)
                act.wait_ge(s_arg[s], 2 * n + 2)
                act.wait_ge(s_coef[s], 2 * n)
                act.activation(e2[s], arg[s], ACT.Exp, scale=-1.0).then_inc(s_exp[s], 1)

            def s_copy(n, s):
                act.wait_ge(s_out[s], n + 1)
                for m in range(2):
                    last = act.activation(
                        H[:, :, bass.ds(2 * SG * n + SG * s, SG), :].rearrange("p q (c m) t -> p m c q t", m=2)[:, m],
                        yp[s][:, m].rearrange("p c (q t) -> p c q t", q=PARTS), ACT.Copy)
                last.then_inc(s_copied[s], 1)

            s_powers(0, 0)
            with act.Fori(0, NSG // 2 - 1) as n:
                s_powers(n, 1)
                s_copy(n, 0)
                s_powers(n + 1, 0)
                s_copy(n, 1)
            s_powers(NSG // 2 - 1, 1)
            s_copy(NSG // 2 - 1, 0)
            s_copy(NSG // 2 - 1, 1)
            for s in range(2):
                act.wait_ge(s_copied[s], NSG // 2)

            for p in range(PARTS):
                with act.Fori(0, GU) as i:
                    n = GU * p + i
                    for s in range(2):
                        act.wait_ge(b_scale[s], B_EXP * n + 2)
                        act.wait_ge(b_sent[s], SENT * n)
                        act.wait_ge(b_dve[s], B_DVE * n)
                        for t in range(GB):
                            last = act.activation(slots[:, 2 + s, t, :],
                                                  H[:, p, :, bass.ds(2 * GB * i + GB * s + t, 1)].rearrange("p c o -> p (c o)"),
                                                  ACT.Identity, scale=norm4[s][2][:, t:t + 1], bias=norm4[s][3][:, t:t + 1])
                        last.then_inc(b_y[s], 1)
                        for t in range(GB):
                            m, at = t % 2, 4 * n + 2 * s + t // 2
                            act.wait_ge(b_tp[m], at + 1)
                            act.wait_ge(b_lt[m], at)
                            act.activation(tTs[m], tp[m], ACT.Copy).then_inc(b_tT[m], 1)

            def m_xcopy(n, s):
                act.wait_ge(m_xp[s], n + 1)
                act.wait_ge(m_h[s], n)
                act.activation(xT[s], px, ACT.Copy).then_inc(m_xT[s], 1)

            def m_silu(n, s):
                act.wait_ge(m_h[s], n + 1)
                act.wait_ge(m_a[s], n)
                act.activation(gate[s], ph[s][:, :, 0:HF], ACT.Silu).then_inc(m_gate[s], 1)

            def m_ocopy(n, s):
                act.wait_ge(m_o[s], n + 1)
                act.wait_ge(m_out[s], 16 * n)
                act.activation(o_b[s], po, ACT.Copy).then_inc(m_oc[s], 1)

            for s in range(2):
                act.wait_ge(b_y[s], GU)
                act.wait_ge(b_dve[s], B_DVE * (NG // 2))
            for p in range(PARTS):
                m_xcopy(MU * p, 0)
                m_silu(MU * p, 0)
                m_xcopy(MU * p, 1)
                with act.Fori(0, MU - 1) as i:
                    n = MU * p + i
                    m_silu(n, 1)
                    m_xcopy(n + 1, 0)
                    m_ocopy(n, 0)
                    m_silu(n + 1, 0)
                    m_xcopy(n + 1, 1)
                    m_ocopy(n, 1)
                m_silu(MU * p + MU - 1, 1)
                m_ocopy(MU * p + MU - 1, 0)
                m_ocopy(MU * p + MU - 1, 1)

            with act.Fori(0, NG // 2) as n:
                for s in range(2):
                    act.wait_ge(f_scale[s], 2 * n + 2)
                    for t in range(GB):
                        last = act.activation(gat[s][:, 1, t, :], gat[s][:, 0, t, :], ACT.Identity,
                                              scale=norm4[s][2][:, t:t + 1], bias=norm4[s][3][:, t:t + 1])
                    last.then_inc(f_z[s], 1)

        @block.vector
        def _(dve):
            def moments(st, tiles, s, w, of):
                for t in range(GB):
                    st(dve.bn_stats(stats[s][w][:, t, :], tiles(t)))
                st.wait()
                apart(dve)
                for t in range(GB):
                    st(dve.bn_aggr(mv[s][w][:, t, :], stats[s][w][:, t, :]))
                st.wait()
                st(dve.tensor_scalar(of[0], mv[s][w][:, :, 1], EPS, None, ALU.add))
                st(dve.tensor_scalar(of[1], mv[s][w][:, :, 0], -1.0, None, ALU.mult))

            dve.wait_ge(exp_ready, 1)
            dve.wait_ge(const_ready, CONSTS)
            st = Steps(dve, table_ready, TABLES, 0)
            pairs = dt_row.rearrange("p (q m) -> p q m", m=2)
            for m in range(2):
                rows = slice(NS * m, NS * m + NS)
                st(dve.tensor_scalar(wd[rows, :], pairs[rows, :, m], a_col[rows, :], None, ALU.mult))
            dve.wait_ge(ct_psum, 1)
            st(dve.tensor_copy(ct, ct_p))
            st(dve.tensor_copy(wgT, wg_p))
            st.wait()
            for m in range(2):
                rows = slice(NS * m, NS * m + NS)
                st(dve.tensor_copy(cz[rows, :, m], ct[rows, :]))
            st.end()

            with dve.Fori(0, NG // 4) as n:
                for s in range(4):
                    dve.wait_ge(a_loaded[s], 16 * (n + 1))
                    st = Steps(dve, a_dve[s], A_DVE, n)
                    moments(st, lambda t: slots[:, s, t, :], s % 2, s // 2, norm4[s])
                    st.end()
                dve.wait_ge(w_psum, n + 1)
                dve.wait_ge(w_stored, 32 * n)
                dve.tensor_copy(wst1[:, 0, :], wp1[:, 0, :])
                dve.tensor_copy(wst1[:, 1, :], wp1[:, 1, :]).then_inc(w_copied, 1)
                dve.tensor_copy(wst2, wp2).then_inc(w_copied, 1)

            for s in range(2):
                dve.wait_ge(k_mm[s], NSG // 2)
                dve.wait_ge(a_done[2 + s], NG // 4)
            st = Steps(dve, k_ready, 5, 0)
            dve.tensor_copy(k_rows, kt_p).then_inc(k_row, 1)
            st(dve.memset(k_pad, 0.0))
            st.wait()
            dve.wait_ge(k_tr, 1)
            for h in range(C // P):
                st(dve.tensor_copy(k_pad[:, h, P - 1:2 * P - 1], kr_p[:, h, :]))
            st.wait()
            for h in range(C // P):
                st(dve.tensor_tensor(k_pad[:, h, P - 1:P], k_pad[:, h, P - 1:P], d_col[:, h:h + 1], ALU.add))
            st.end()

            dve.wait_ge(w_stored, 32 * E)
            with dve.Fori(0, NSG // 2) as n:
                for s in range(2):
                    dve.wait_ge(s_exp[s], 2 * n + 2)
                    dve.wait_ge(s_out[s], n)
                    dve.tensor_tensor(e2c[s], e2[s][:, :, 1:P + 1],
                                      ct[:, bass.ds(2 * PR * n + PR * s, PR)].unsqueeze(2).broadcast_to([P, PR, P]),
                                      ALU.mult).then_inc(s_coef[s], 1)
                    dve.tensor_tensor(decay[s].rearrange("p (q t) -> p q t", q=PR), decay_mask.unsqueeze(1).broadcast_to([P, PR, NT]),
                                      e2[s][:, :, P:P + 1].broadcast_to([P, PR, NT]), ALU.mult).then_inc(s_coef[s], 1)
                    dve.wait_ge(s_in[s], n + 1)
                    dve.wait_ge(s_coef[s], 2 * n + 2)
                    dve.tensor_tensor_scan(state[s].rearrange("p q t -> p (q t)"), decay[s], xp[s].rearrange("p q t -> p (q t)"),
                                           0.0, ALU.mult, ALU.add).then_inc(s_state[s], 1)

            def bt(v):
                return v.unsqueeze(2).broadcast_to([P, GB, E])

            def be(v):
                return v.unsqueeze(1).broadcast_to([P, GB, E])

            def route(p, i, s):
                n = GU * p + i
                st = Steps(dve, b_dve[s], B_DVE, n)
                x, rows = slots[:, s], slots[:, 2 + s]
                at = 2 * GB * n + GB * s
                moments(st, lambda t: H[:, p, :, bass.ds(2 * GB * i + GB * s + t, 1)].rearrange("p c o -> p (c o)"), s, 0, norm4[s])
                assert st.done == B_VAR1
                dve.wait_ge(b_x[s], 16 * (n + 1))
                dve.wait_ge(b_y[s], n + 1)
                st(dve.tensor_tensor(x, x, rows, ALU.add))
                assert st.done == B_SUM
                st.wait()
                moments(st, lambda t: x[:, t, :], s, 1, norm8[s])
                assert st.done == B_VAR2
                dve.wait_ge(b_scale[s], B_EXP * n + 4)
                for t in range(GB):
                    st(dve.tensor_scalar(rows[:, t, :], x[:, t, :], norm8[s][2][:, t:t + 1], norm8[s][3][:, t:t + 1], ALU.mult, ALU.add))
                assert st.done == B_ROWS
                for m in range(2):
                    dve.wait_ge(b_lt[m], 4 * n + 2 * s + 2)
                st(dve.tensor_tensor(lg[s], lp[s], be(bg_row), ALU.add))
                st.wait()
                st(dve.tensor_reduce(best[s], lg[s], AX.X, ALU.max))
                st.wait()
                st(dve.tensor_tensor(tmp[s], lg[s], bt(best[s]), ALU.is_equal))
                st.wait()
                st(dve.tensor_tensor(tmp2[s], tmp[s], be(rev_e), ALU.mult))
                st.wait()
                st(dve.tensor_reduce(pick[s], tmp2[s], AX.X, ALU.max))
                st.wait()
                st(dve.tensor_tensor(oh1[s], be(rev_e), bt(pick[s]), ALU.is_equal))
                st.wait()
                st(dve.scalar_tensor_tensor(lg2[s], oh1[s], -1e30, lg[s], ALU.mult, ALU.add))
                st.wait()
                st(dve.tensor_reduce(best2[s], lg2[s], AX.X, ALU.max))
                st.wait()
                st(dve.tensor_tensor(gap[s], best2[s], best[s], ALU.subtract))
                assert st.done == B_GAP
                st(dve.tensor_tensor(tmp[s], lg2[s], bt(best2[s]), ALU.is_equal))
                st.wait()
                st(dve.tensor_tensor(tmp2[s], tmp[s], be(rev_e), ALU.mult))
                st.wait()
                st(dve.tensor_reduce(pick[s], tmp2[s], AX.X, ALU.max))
                st.wait()
                st(dve.tensor_tensor(oh2[s], be(rev_e), bt(pick[s]), ALU.is_equal))
                st.wait()
                by_tile = chosen[s].rearrange("p (e t) -> p t e", e=E)
                st(dve.tensor_tensor(by_tile, oh1[s], oh2[s], ALU.add))
                st.wait()
                st(dve.tensor_tensor_scan(seen[s], scan_keep, chosen[s], 0.0, ALU.mult, ALU.add))
                assert st.done == B_SEEN
                st.wait()
                st(dve.tensor_tensor(pos[s], seen[s].rearrange("p (e t) -> p t e", e=E), by_tile, ALU.subtract))
                dve.wait_ge(b_rank[s], n + 1)
                st(dve.tensor_tensor(rank_base[s], rp[s][:, 0:E], run, ALU.add))
                st.wait()
                st(dve.tensor_tensor(pos[s], pos[s], be(rank_base[s]), ALU.add))
                st(dve.tensor_tensor(run, rp[s][:, E:2 * E], run, ALU.add))
                st.wait()
                st(dve.tensor_tensor(tmp[s], oh1[s], pos[s], ALU.mult))
                st(dve.tensor_tensor(tmp2[s], oh2[s], pos[s], ALU.mult))
                st.wait()
                st(dve.tensor_reduce(slot_tab[:, 0, bass.ds(at, GB)], tmp[s], AX.X, ALU.add))
                st(dve.tensor_reduce(slot_tab[:, 1, bass.ds(at, GB)], tmp2[s], AX.X, ALU.add))
                st.wait()
                dve.wait_ge(b_sent[s], SENT * n)
                st(dve.tensor_scalar(idx[s], slot_tab[:, :, bass.ds(at, GB)], 0.0, None, ALU.add))
                assert st.done == B_IDX
                dve.wait_ge(b_scale[s], B_EXP * n + 5)
                st(dve.tensor_scalar(wsum[s], eg[s], 1.0, None, ALU.add))
                st.wait()
                st(dve.reciprocal(w_tab[:, 0, bass.ds(at, GB)], wsum[s]))
                st.wait()
                st(dve.tensor_tensor(w_tab[:, 1, bass.ds(at, GB)], w_tab[:, 0, bass.ds(at, GB)], eg[s], ALU.mult))
                st.end()
                st.wait()

            def tile_table(p):
                st = Steps(dve, q_dve, Q_DVE, p)
                if p:
                    dve.wait_ge(q_padded, 16 * E * p)
                st(dve.tensor_tensor(counts, run, cap_base, ALU.subtract))
                st(dve.tensor_scalar(idx_pad, run, part_no, None, ALU.add))
                st.wait()
                st(dve.tensor_tensor(over, counts.unsqueeze(2).broadcast_to([P, E, TP]), steps_k.unsqueeze(1).broadcast_to([P, E, TP]), ALU.is_gt))
                st.wait()
                st(dve.tensor_reduce(ntile, over, AX.X, ALU.add))
                st.wait()
                st(dve.tensor_tensor_scan(ends, ones[:, 0:E], ntile, 0.0, ALU.mult, ALU.add))
                st.wait()
                st(dve.tensor_tensor(starts, ends, ntile, ALU.subtract))
                st(dve.tensor_scalar(last_t, ends[:, E - 1:E], -1.0, None, ALU.add))
                st.wait()
                st(dve.tensor_scalar(t_at, tile_no, last_t, None, ALU.min))
                st(dve.scalar_tensor_tensor(delta, starts, float(P), cap_base, ALU.mult, ALU.subtract))
                st.wait()
                st(dve.tensor_tensor(g_e, t_at.unsqueeze(2).broadcast_to([P, MT, E - 1]), ends[:, 0:E - 1].unsqueeze(1).broadcast_to([P, MT, E - 1]), ALU.is_ge))
                st.wait()
                st(dve.tensor_reduce(e_of, g_e, AX.X, ALU.add))
                st.wait()
                st(dve.tensor_tensor(g_e, g_e, ends[:, 0:E - 1].unsqueeze(1).broadcast_to([P, MT, E - 1]), ALU.mult))
                st.wait()
                st(dve.tensor_reduce(st_of, g_e, AX.X, ALU.max))
                st(dve.tensor_tensor(step_d[:, 1:E], delta[:, 1:E], delta[:, 0:E - 1], ALU.subtract))
                st(dve.tensor_copy(run, cap_base))
                st.wait()
                st(dve.tensor_tensor(t_at, t_at, st_of, ALU.subtract))
                st.wait()
                st(dve.scalar_tensor_tensor(in_tile[:, p, :], e_of, float(CAPT), t_at, ALU.mult, ALU.add))
                st(dve.tensor_copy(tile_e[:, p, :], e_of))
                of_part = slot_tab[:, :, TP * p:TP * p + TP]
                steps = g_e.rearrange("p t e -> p (t e)")[:, 0:K2 * TP * (E - 1)].rearrange("p (k t e) -> p k t e", k=K2, e=E - 1)
                for_all = cap_base[:, 1:E].unsqueeze(1).unsqueeze(1).broadcast_to([P, K2, TP, E - 1])
                st(dve.tensor_tensor(steps, of_part.unsqueeze(3).broadcast_to([P, K2, TP, E - 1]), for_all, ALU.is_ge))
                st.wait()
                st(dve.tensor_tensor(steps, steps, step_d[:, 1:E].unsqueeze(1).unsqueeze(1).broadcast_to([P, K2, TP, E - 1]), ALU.mult))
                st.wait()
                st(dve.tensor_reduce(shift, steps, AX.X, ALU.add))
                st.wait()
                st(dve.tensor_tensor(slot_tab_i[:, :, TP * p:TP * p + TP], of_part, shift, ALU.add))
                st.end()
                st.wait()

            for s in range(2):
                dve.wait_ge(s_copied[s], NSG // 2)
            for p in range(PARTS):
                with dve.Fori(0, GU) as i:
                    for s in range(2):
                        route(p, i, s)
                tile_table(p)

            def m_mul(n, s):
                dve.wait_ge(m_gate[s], n + 1)
                dve.wait_ge(m_ap[s], n)
                dve.tensor_tensor(act_b[s], gate[s], ph[s][:, :, HF:DFF], ALU.mult).then_inc(m_a[s], 1)

            def m_acopy(n, s):
                dve.wait_ge(m_ap[s], n + 1)
                dve.wait_ge(m_o[s], n)
                dve.tensor_copy(aT[s], pa).then_inc(m_aT[s], 1)

            for p in range(PARTS):
                m_mul(MU * p, 0)
                with dve.Fori(0, MU - 1) as i:
                    n = MU * p + i
                    m_acopy(n, 0)
                    m_mul(n, 1)
                    m_acopy(n, 1)
                    m_mul(n + 1, 0)
                m_acopy(MU * p + MU - 1, 0)
                m_mul(MU * p + MU - 1, 1)
                m_acopy(MU * p + MU - 1, 1)

            with dve.Fori(0, NG // 2) as n:
                for s in range(2):
                    st = Steps(dve, f_dve[s], F_DVE, n)
                    at = 2 * GB * n + GB * s
                    dve.wait_ge(f_got[s], SENT * (n + 1))
                    for t in range(GB):
                        st(dve.tensor_scalar(gat[s][:, 0, t, :], gat[s][:, 0, t, :], w_tab[:, 0, bass.ds(at + t, 1)], None, ALU.mult))
                    st.wait()
                    for t in range(GB):
                        st(dve.scalar_tensor_tensor(gat[s][:, 0, t, :], gat[s][:, 1, t, :], w_tab[:, 1, bass.ds(at + t, 1)],
                                                    gat[s][:, 0, t, :], ALU.mult, ALU.add))
                    st.wait()
                    moments(st, lambda t: gat[s][:, 0, t, :], s, 0, norm4[s])
                    dve.wait_ge(f_x[s], 16 * (n + 1))
                    dve.wait_ge(f_z[s], n + 1)
                    st(dve.tensor_tensor(fx[s], fx[s], gat[s][:, 1], ALU.add))
                    st.end()

        @block.tensor
        def _(pe):
            pe.wait_ge(const_ready, CONSTS)
            pe.wait_ge(const_in, 16 * 9)
            pe.transpose(ct_p, c_rows, ident)
            for k in range(KC):
                last = pe.transpose(wg_p[:, k, :], wg_rows[0:E, P * k:P * k + P], ident[0:E, 0:E])
            last.then_inc(ct_psum, 1)

            pe.wait_ge(table_ready, TABLES)
            with pe.Fori(0, NG // 4) as n:
                for s in range(4):
                    k, kn = s % 2, 2 * n + s // 2
                    pe.wait_ge(k_exp[k], kn + 1)
                    for q in range(PR):
                        last = pe.matmul(kt_p[:, bass.ds(4 * SG * n + SG * s + 2 * q, 2)], e2[k][:, q, 0:P],
                                         cz[:, bass.ds(4 * PR * n + PR * s + q, 1), :].rearrange("p o m -> p (o m)"), start=True, stop=True)
                    last.then_inc(k_mm[k], 1)
                pe.wait_ge(w_loaded, 32 * (n + 1))
                pe.wait_ge(w_copied, 2 * n)
                for k in range(KC):
                    for j in range(DFF // P):
                        pe.transpose(wp1[:, k, P * j:P * j + P], wrow1[:, j, P * k:P * k + P], ident)
                    for j in range(C // P):
                        last = pe.transpose(wp2[:, k, P * j:P * j + P], wrow2[:, j, P * k:P * k + P], ident)
                last.then_inc(w_psum, 1)
            pe.wait_ge(k_row, 1)
            for h in range(C // P):
                last = pe.transpose(kr_p[:, h, :], k_rows[:, P * h:P * h + P], ident)
            last.then_inc(k_tr, 1)

            for s in range(4):
                pe.wait_ge(a_done[s], NG // 4)
            pe.wait_ge(w_copied, 2 * E)

            def channel(m):
                return H[:, :, bass.ds(m, 1), :].rearrange("p q o t -> p q (o t)")

            def s_inputs(n, s):
                pe.wait_ge(s_exp[s], 2 * n + 1)
                pe.wait_ge(s_state[s], n)
                for q in range(PR):
                    for m in range(2):
                        last = pe.matmul(xp[s][:, q, :].rearrange("p (q t) -> p q t", q=PARTS), e1[s][:, q, NS * m:NS * m + P],
                                         channel(2 * SG * n + SG * s + 2 * q + m), start=(m == 0), stop=(m == 1))
                last.then_inc(s_in[s], 1)

            def s_outputs(n, s):
                pe.wait_ge(s_toep[s], 16 * (n + 1))
                pe.wait_ge(s_coef[s], 2 * n + 1)
                pe.wait_ge(s_state[s], n + 1)
                pe.wait_ge(s_copied[s], n)
                for q in range(PR):
                    for m in range(2):
                        y = yp[s][:, m, q, :]
                        rows = slice(NS * m, NS * m + NS)
                        pe.matmul(y.rearrange("p (q t) -> p q t", q=PARTS), toep[s][:, 2 * q + m, :], channel(2 * SG * n + SG * s + 2 * q + m),
                                  start=True, stop=False)
                        last = pe.matmul(y.rearrange("p (b a) -> p b a", a=CH)[:, :, 1:CH], e2c[s][rows, q, :],
                                         state[s][rows, q, :].rearrange("p (b a) -> p b a", a=CH)[:, :, 0:CH - 1], start=False, stop=True)
                last.then_inc(s_out[s], 1)

            s_inputs(0, 0)
            with pe.Fori(0, NSG // 2 - 1) as n:
                s_inputs(n, 1)
                s_outputs(n, 0)
                s_inputs(n + 1, 0)
                s_outputs(n, 1)
            s_inputs(NSG // 2 - 1, 1)
            s_outputs(NSG // 2 - 1, 0)
            s_outputs(NSG // 2 - 1, 1)

            for s in range(2):
                pe.wait_ge(s_copied[s], NSG // 2)

            def b_transpose(n, s, t):
                m, at = t % 2, 4 * n + 2 * s + t // 2
                pe.wait_ge(b_dve[s], B_DVE * n + B_VAR2 + 1 + t)
                pe.wait_ge(b_tT[m], at)
                for k in range(KC):
                    last = pe.transpose(tp[m][:, k, :], slots[:, 2 + s, t, P * k:P * k + P], ident)
                last.then_inc(b_tp[m], 1)

            def b_logits(n, s, t):
                m, at = t % 2, 4 * n + 2 * s + t // 2
                pe.wait_ge(b_tT[m], at + 1)
                for k in range(KC):
                    last = pe.matmul(lp[s][:, t, :], tTs[m][:, k, :], wgT[:, k, :], start=(k == 0), stop=(k == KC - 1))
                last.then_inc(b_lt[m], 1)

            with pe.Fori(0, NG // 2) as n:
                for s in range(2):
                    b_transpose(n, s, 0)
                    for t in range(1, GB):
                        b_transpose(n, s, t)
                        b_logits(n, s, t - 1)
                    b_logits(n, s, GB - 1)
                    pe.wait_ge(b_dve[s], B_DVE * n + B_SEEN)
                    for v, w in ((before, 0), (ones, 1)):
                        last = pe.matmul(rp[s][:, E * w:E * w + E], v, seen[s].rearrange("p (e t) -> p e t", e=E)[:, :, GB - 1],
                                         start=True, stop=True)
                    last.then_inc(b_rank[s], 1)

            pe.wait_ge(weights_in, 32)

            def expert(p, j, t):
                return pe.value_load(tile_e[0:1, p, bass.ds(2 * j + t, 1)], min_val=0, max_val=E - 1)

            def m_xtr(n, s):
                pe.wait_ge(m_in[s], 32 * (n + 1))
                pe.wait_ge(m_xT[1 - s], n + s)
                for t in range(2):
                    for k in range(KC):
                        last = pe.transpose(px[:, t, k, :], xin[s][:, t, P * k:P * k + P], ident)
                last.then_inc(m_xp[s], 1)

            def m_up(p, j, n, s):
                of_tile = [expert(p, j, t) for t in range(2)]
                pe.wait_ge(m_xT[s], n + 1)
                pe.wait_ge(m_a[s], n)
                for t, e in enumerate(of_tile):
                    for k in range(KC):
                        last = pe.matmul(ph[s][:, t, :], xT[s][:, t, k, :], W1[:, k, bass.ds(e, 1), :].rearrange("p o n -> p (o n)"),
                                         start=(k == 0), stop=(k == KC - 1))
                last.then_inc(m_h[s], 1)

            def m_atr(n, s):
                pe.wait_ge(m_a[s], n + 1)
                pe.wait_ge(m_aT[1 - s], n + s)
                for t in range(2):
                    for k in range(KC):
                        last = pe.transpose(pa[:, t, k, :], act_b[s][:, t, P * k:P * k + P], ident)
                last.then_inc(m_ap[s], 1)

            def m_down(p, j, n, s):
                of_tile = [expert(p, j, t) for t in range(2)]
                pe.wait_ge(m_aT[s], n + 1)
                pe.wait_ge(m_oc[1 - s], n + s)
                for t, e in enumerate(of_tile):
                    for k in range(KC):
                        last = pe.matmul(po[:, t, :], aT[s][:, t, k, :], W2[:, k, bass.ds(e, 1), :].rearrange("p o n -> p (o n)"),
                                         start=(k == 0), stop=(k == KC - 1))
                last.then_inc(m_o[s], 1)

            for p in range(PARTS):
                pe.wait_ge(q_dve, Q_DVE * (p + 1))
                m_xtr(MU * p, 0)
                m_up(p, 0, MU * p, 0)
                m_xtr(MU * p, 1)
                with pe.Fori(0, MU - 1) as i:
                    n = MU * p + i
                    m_up(p, 2 * i + 1, n, 1)
                    m_atr(n, 0)
                    m_xtr(n + 1, 0)
                    m_down(p, 2 * i, n, 0)
                    m_up(p, 2 * i + 2, n + 1, 0)
                    m_atr(n, 1)
                    m_xtr(n + 1, 1)
                    m_down(p, 2 * i + 1, n, 1)
                n = MU * p + MU - 1
                m_up(p, MP - 1, n, 1)
                m_atr(n, 0)
                m_down(p, MP - 2, n, 0)
                m_atr(n, 1)
                m_down(p, MP - 1, n, 1)


_INS = ["L0_attn_u", "L0_attn_A_log", "L0_attn_D", "L0_attn_C_re", "L0_attn_log_dt",
        "L0_ffn_Wg", "L0_ffn_bg", "L0_ffn_w1", "L0_ffn_w2"]
_OUTS = [((B, L, C), "float32")]


def kernel(**inputs):
    import concourse.bacc as _bacc
    from concourse.bass_utils import run_bass_kernel_spmd as _run

    nc = _bacc.Bacc("TRN2", target_bir_lowering=False, num_devices=1)
    arrays, args = {}, []
    for name in _INS:
        a = np.ascontiguousarray(inputs[name])
        arrays[f"in_{name}_dram"] = a
        args.append(nc.dram_tensor(f"in_{name}_dram", a.shape, mybir.dt.from_np(a.dtype), kind="ExternalInput").ap())
    for i, (shape, dtype) in enumerate(_OUTS):
        args.append(nc.dram_tensor(f"out_{i}_dram", shape, mybir.dt.from_np(np.dtype(dtype)), kind="ExternalOutput").ap())
    ssm_moe_block(nc, *args)
    r = _run(nc, [arrays], core_ids=[0])
    return r.results[0]["out_0_dram"]
```

```python
from contextlib import ExitStack

import numpy as np
import concourse.bass as bass
from concourse import mybir

F32 = mybir.dt.float32
I32 = mybir.dt.int32
ALU = mybir.AluOpType
ACT = mybir.ActivationFunctionType
AX = mybir.AxisListType
PE, SP = mybir.EngineType.PE, mybir.EngineType.SP

P = 128
B, L, C = 8, 2048, 256
NS = 64
E, K2 = 8, 2
DFF = 512
HF = DFF // 2
CH = L // P
NT = B * CH
KC = C // P
GB = 4
NG = NT // GB
PARTS = 4
GP = NG // PARTS
TP = NT // PARTS
CAPT = TP + 1
CAPR = CAPT * P
MT = TP * K2 + E
MP = MT // 2
SG = 8
NSG = C // SG
PR = SG // 2
NQ = 8
EPS = 1e-5


class Steps:

    def __init__(self, engine, sem, per, at, done=0):
        self.engine, self.sem, self.per, self.at, self.done = engine, sem, per, at, done

    def __call__(self, instruction):
        instruction.then_inc(self.sem, 1)
        self.done += 1

    def wait(self):
        self.engine.wait_ge(self.sem, self.at * self.per + self.done)

    def end(self):
        assert self.done == self.per, (self.done, self.per)


def ssm_moe_block(nc, u, A_log, D, C_re, log_dt, Wg, bg, w1, w2, out):
    ctx = ExitStack()
    with ctx:
        def sem(name):
            return ctx.enter_context(nc.semaphore(name))

        def sems(name, n=2):
            return [sem(f"{name}{i}") for i in range(n)]

        def region(name, words, dt=F32):
            return ctx.enter_context(nc.sbuf_tensor(name, [P, words], dt))

        class Carve:

            def __init__(self, base, size):
                self.base, self.size, self.at = base, size, 0

            def take(self, *shape):
                n = int(np.prod(shape))
                v = self.base[:, self.at:self.at + n]
                self.at += n
                assert self.at <= self.size, (self.at, self.size)
                names = " ".join(f"d{i}" for i in range(len(shape)))
                if len(shape) == 1:
                    return v
                return v.rearrange(f"p ({names}) -> p {names}", **{f"d{i}": s for i, s in enumerate(shape)})

            def two(self, *shape):
                return [self.take(*shape), self.take(*shape)]

        def scratch(name, shape):
            return nc.dram_tensor(name, shape, F32, kind="Internal").ap()

        toep_dram = scratch("toeplitz", (C, P, P))
        w1_dram = scratch("w1_transposed", (P, KC, E, DFF))
        w2_dram = scratch("w2_transposed", (P, KC, E, C))
        x2_dram = scratch("x_after_ssm", (NT * P, C))
        list_dram = [scratch(f"expert_rows{p}", (E * CAPR, C)) for p in range(PARTS)]
        eo_dram = [scratch(f"expert_out{p}", (MT * P, C)) for p in range(PARTS)]
        u_rows = u.rearrange("b (a p) c -> p (b a) c", p=P)
        x2_rows = x2_dram.rearrange("(t p) c -> p t c", p=P)
        out_rows = out.rearrange("b (a p) c -> p (b a) c", p=P)

        PSZ = C * TP
        hid = region("hid", PARTS * PSZ)
        H = hid[:, :].rearrange("p (q c t) -> p q c t", q=PARTS, c=C)
        wide_size = E * KC * (DFF + C)
        wide = region("wide", wide_size)
        group = region("group", 4 * GB * C)
        slots = group[:, :].rearrange("p (s t c) -> p s t c", s=4, t=GB)
        small = Carve(region("small", 3720), 3720)
        ident = small.take(P)
        before = small.take(P)
        ones = small.take(P)
        minus_half = small.take(GB)
        e_base = small.take(GB)
        part_no = small.take(1)
        rev_e = small.take(E)
        cap_base = small.take(E)
        scan_keep = small.take(E * GB)
        wgT = small.take(KC, E)
        bg_row = small.take(E)
        tTs = small.two(2, KC, P)
        stats = [small.two(GB, 6) for _ in range(3)]
        mv = [small.two(GB, 2) for _ in range(3)]
        norm4 = [[small.take(GB) for _ in range(4)] for _ in range(4)]
        norm8 = [[small.take(GB) for _ in range(4)] for _ in range(2)]
        lg, lg2, tmp, tmp2, oh1, oh2, pos = [small.two(GB, E) for _ in range(7)]
        best, best2, pick, gap, eg, wsum = [small.two(GB) for _ in range(6)]
        chosen, seen = [small.two(E * GB) for _ in range(2)]
        rank_base = small.two(E)
        run = small.take(E)
        w_tab = small.take(K2, NT)
        slot_tab = small.take(K2, NT)
        small_i = Carve(region("small_i", 320, I32), 320)
        slot_tab_i = small_i.take(K2, NT)
        idx = small_i.two(K2, GB)
        idx_f = small_i.two(K2, GB)
        idx_pad = small_i.take(E)
        mb = Carve(hid[:, 0:PSZ], PSZ)
        xin = mb.two(2, C)
        xT = mb.two(2, KC, P)
        gate = mb.two(2, HF)
        act_b = mb.two(2, HF)
        aT = mb.two(2, KC, P)
        o_b = mb.two(2, C)
        tabs_i = Carve(mb.take(2 * PARTS * MT).bitcast(I32), 2 * PARTS * MT)
        in_tile = tabs_i.take(PARTS, MT)
        tile_e = tabs_i.take(PARTS, MT)
        tabs = mb
        over = tabs.take(E, TP)
        zero_row = tabs.take(C)
        tile_no = tabs.take(MT)
        steps_k = tabs.take(TP)
        counts, ntile, ends, starts, delta, step_d = [tabs.take(E) for _ in range(6)]
        last_t = tabs.take(1)
        t_at, e_of, st_of = [tabs.take(MT) for _ in range(3)]
        g_e = tabs.take(MT, E - 1)
        shift = over.rearrange("p e t -> p (e t)")[:, 0:K2 * TP].rearrange("p (k t) -> p k t", k=K2)

        wb = Carve(wide, wide_size)
        toep = wb.two(SG, P)
        vrow = wb.two(PR, 2, NS)
        arg = wb.two(PR, P + 1)
        e1 = wb.two(PR, 3 * NS)
        e2 = wb.two(PR, P + 1)
        wb_e2c = wb.at
        e2c = wb.two(PR, P)
        decay = wb.two(PR * NT)
        wb_state = wb.at
        state = wb.two(PR, NT)
        iota_l = wb.take(P + 1)
        decay_mask = wb.take(NT)
        rev_pos = wb.take(1)
        dt_row = wb.take(C)
        a_row = wb.take(NS)
        a_col = wb.take(1)
        wd = wb.take(C // 2)
        ct = wb.take(C // 2)
        d_col = wb.take(C // P)
        W1v = Carve(wide, wide_size)
        W1 = W1v.take(KC, E, DFF)
        W2 = W1v.take(KC, E, C)
        fb = Carve(hid[:, PSZ:2 * PSZ], PSZ)
        fx = fb.two(GB, C)
        gat = fb.two(K2, GB, C)
        pro = Carve(wide, 2 * SG * P)
        wrow1 = pro.take(DFF // P, C)
        wst1 = pro.take(KC, DFF)
        pro = Carve(wide[:, wb_e2c:], 2 * PR * P)
        wrow2 = pro.take(C // P, C)
        wst2 = pro.take(KC, C)
        pro = Carve(wide[:, wb_state:], 2 * PR * NT)
        cz = pro.take(C // 2, 2)
        c_rows = pro.take(P)
        wg_rows = pro.take(C)
        k_rows = slots[:, 2, 0, :]
        k_pad = slots[:, 3, 0:C // P, :]

        banks = ctx.enter_context(nc.psum_tensor("banks", [P, 8 * 512], F32))

        def bank(i, n=1):
            return banks[:, 512 * i:512 * (i + n)]

        xp = [bank(i).rearrange("p (q t) -> p q t", q=PR) for i in range(2)]
        yp = [bank(2 + 2 * i, 2).rearrange("p (m q t) -> p m q t", m=2, q=PR) for i in range(2)]
        kt_p = bank(6)[:, 0:C]
        ct_p = bank(7)[:, 0:P]
        wg_p = bank(7)[:, P:P + KC * E].rearrange("p (k e) -> p k e", k=KC)
        kr_p = bank(7)[:, 0:C].rearrange("p (h l) -> p h l", h=C // P)
        wp1 = bank(0, 2).rearrange("p (k n) -> p k n", k=KC)
        wp2 = bank(2).rearrange("p (k n) -> p k n", k=KC)
        ph = [bank(2 * i, 2).rearrange("p (t n) -> p t n", t=2) for i in range(2)]
        px = bank(4).rearrange("p (t k n) -> p t k n", t=2, k=KC)
        pa = bank(5).rearrange("p (t k n) -> p t k n", t=2, k=KC)
        po = bank(6).rearrange("p (t n) -> p t n", t=2)
        tp = [px, pa]
        lp = [bank(7)[:, GB * E * i:GB * E * i + GB * E].rearrange("p (t e) -> p t e", t=GB) for i in range(2)]
        rp = [bank(7)[:, 2 * GB * E + 2 * E * i:2 * GB * E + 2 * E * i + 2 * E] for i in range(2)]

        passed = sem("passed")
        const_in, const_ready, exp_ready, table_ready, ct_psum = (
            sem("const_in"), sem("const_ready"), sem("exp_ready"), sem("table_ready"), sem("ct_psum"))
        a_loaded, a_dve, a_scale, a_done = sems("a_loaded", 4), sems("a_dve", 4), sems("a_scale", 4), sems("a_done", 4)
        k_arg, k_exp, k_mm = sems("k_arg"), sems("k_exp"), sems("k_mm")
        k_row, k_tr, k_ready, t_stored = sem("k_row"), sem("k_tr"), sem("k_ready"), sems("t_stored", NQ)
        w_loaded, w_psum, w_copied, w_stored = sem("w_loaded"), sem("w_psum"), sem("w_copied"), sem("w_stored")
        s_toep, s_arg, s_exp, s_coef = sems("s_toep"), sems("s_arg"), sems("s_exp"), sems("s_coef")
        s_in, s_state, s_out, s_copied = sems("s_in"), sems("s_state"), sems("s_out"), sems("s_copied")
        weights_in, tabs_ready = sem("weights_in"), sem("tabs_ready")
        b_x, b_saved, b_dve, b_scale, b_y = sems("b_x"), sems("b_saved"), sems("b_dve"), sems("b_scale"), sems("b_y")
        b_tp, b_tT, b_lt, b_rank, b_sent = sems("b_tp"), sems("b_tT"), sems("b_lt"), sem("b_rank"), sems("b_sent")
        q_dve, q_padded = sem("q_dve"), sem("q_padded")
        m_in, m_xp, m_xT, m_h, m_gate, m_a = (
            sems("m_in"), sems("m_xp"), sems("m_xT"), sems("m_h"), sems("m_gate"), sems("m_a"))
        m_ap, m_aT, m_o, m_oc, m_out = sems("m_ap"), sems("m_aT"), sems("m_o"), sems("m_oc"), sems("m_out")
        f_x, f_idx, f_got, f_dve, f_scale, f_z, f_saved = (
            sems("f_x"), sems("f_idx"), sems("f_got"), sems("f_dve"), sems("f_scale"), sems("f_z"), sems("f_saved"))

        def apart(engine):
            engine.sem_inc(passed, 1)

        CONSTS = 20
        TABLES = 6
        A_DVE = 10
        B_DVE = 53
        Q_DVE = 22
        F_DVE = 20
        B_VAR1, B_BIAS, B_SUM, B_VAR2, B_ROWS, B_LG, B_GAP, B_SEEN, B_RANK, B_IDX = 10, 11, 12, 22, 26, 27, 35, 41, 44, 50
        F_SUM, F_VAR, F_BIAS = 8, 18, 19
        B_EXP = 3
        GU = GP // 2
        MU = MP // 2
        SENT = 16 * K2 * GB
        CY = 8
        NCY = GP // 2

        def after(engine, sem_, value):
            if not (isinstance(value, int) and value == 0):
                engine.wait_ge(sem_, value)

        def cycles(engine, cycle, m, b, f):
            first = m == 0 or b == 0 or f == 0
            if first:
                cycle(0, m, b, f)
            with engine.Fori(0, NCY - first) as i:
                cycle(i + 1 if first else i, m, b, f)

        class Pair:

            def __init__(self, p, i, c):
                self.p, self.s, self.u, self.j = p, c % 2, MU * p + CY // 2 * i + c // 2, CY * i + c
        block = ctx.enter_context(nc.Block())

        @block.sync
        def _(sp):
            sp.dma_start(a_col[0:NS, :], A_log.rearrange("(n o) -> n o", o=1)).then_inc(const_in, 16)
            sp.dma_start(a_col[NS:2 * NS, :], A_log.rearrange("(n o) -> n o", o=1)).then_inc(const_in, 16)
            sp.dma_start(a_row, A_log.partition_broadcast(P)).then_inc(const_in, 16)
            sp.dma_start(dt_row, log_dt.partition_broadcast(P)).then_inc(const_in, 16)
            sp.dma_start(c_rows, C_re.rearrange("(p m) n -> p (m n)", m=2)).then_inc(const_in, 16)
            for h in range(C // P):
                sp.dma_start(d_col[:, h:h + 1], D[P * h:P * h + P].rearrange("(p o) -> p o", o=1)).then_inc(const_in, 16)
            sp.dma_start(wg_rows[0:E, :], Wg).then_inc(const_in, 16)
            sp.dma_start(bg_row, bg.partition_broadcast(P)).then_inc(const_in, 16)

            with sp.Fori(0, NG // 4) as n:
                for s in range(4):
                    sp.wait_ge(a_done[s], n)
                    sp.dma_start(slots[:, s], u_rows[:, bass.ds(4 * GB * n + GB * s, GB), :]).then_inc(a_loaded[s], 16)
                sp.wait_ge(w_psum, n)
                sp.dma_start(wrow1, w1.rearrange("e (j p) k -> p e j k", p=P)[:, bass.ds(n, 1)].rearrange("p o j k -> p (o j) k")).then_inc(w_loaded, 16)
                sp.dma_start(wrow2, w2.rearrange("e (j p) k -> p e j k", p=P)[:, bass.ds(n, 1)].rearrange("p o j k -> p (o j) k")).then_inc(w_loaded, 16)
            sp.wait_ge(k_ready, 5)
            for q in range(NQ):
                h, rows = q // (NQ // 2), slice(C // NQ * (q % (NQ // 2)), C // NQ * (q % (NQ // 2)) + C // NQ)
                v = k_pad[rows, h, P - 1:2 * P - 1]
                skew = bass.AP(v.tensor, v.offset, [v.ap[0], [-1, P], [1, P]])
                sp.dma_start(toep_dram[C // NQ * q:C // NQ * q + C // NQ], skew).then_inc(t_stored[q], 16)
            sp.wait_ge(w_stored, 32 * E)
            for g in range(NSG):
                sp.wait_ge(t_stored[SG * g * NQ // C], 16)
                if g >= 2:
                    sp.wait_ge(s_out[g % 2], g // 2)
                sp.dma_start(toep[g % 2], toep_dram[SG * g:SG * g + SG].rearrange("c j i -> j c i")).then_inc(s_toep[g % 2], 16)
            for s in range(2):
                sp.wait_ge(s_copied[s], NSG // 2)
            sp.dma_start(W1, w1_dram).then_inc(weights_in, 16)
            sp.dma_start(W2, w2_dram).then_inc(weights_in, 16)

            def b_load(n, s):
                after(sp, b_saved[s], 16 * n)
                if not isinstance(n, int):
                    apart(sp)
                after(sp, b_dve[s], B_DVE * n)
                sp.dma_start(slots[:, s], u_rows[:, bass.ds(2 * GB * n + GB * s, GB), :]).then_inc(b_x[s], 16)

            def b_save(n, s):
                sp.wait_ge(b_dve[s], B_DVE * n + B_SUM)
                sp.dma_start(x2_rows[:, bass.ds(2 * GB * n + GB * s, GB), :], slots[:, s]).then_inc(b_saved[s], 16)

            def m_load(pair, tiles):
                after(sp, m_xp[pair.s], pair.u)
                if not isinstance(pair.u, int):
                    apart(sp)
                lists = list_dram[pair.p].rearrange("(n r) c -> n r c", r=P)
                for t, at in enumerate(tiles):
                    sp.dma_start(xin[pair.s][:, t, :], lists[bass.ds(at, 1)].rearrange("o r c -> r (o c)")).then_inc(m_in[pair.s], 16)

            def two_pairs(p, i, c):
                v = nc.values_load_multi_w_load_instructions(in_tile[0:1, p, bass.ds(2 * CY * i + 2 * c, 4)], engines=(SP,),
                                                             min_val=0, max_val=E * CAPT - 1)[1]
                return {c: v[0:2], c + 1: v[2:4]}

            def m_first(p):
                sp.wait_ge(q_dve, Q_DVE * (p + 1))
                sp.wait_ge(q_padded, 16 * E * (p + 1))
                for s in range(2):
                    sp.wait_ge(b_sent[s], SENT * GU * (p + 1))
                tiles = two_pairs(p, 0, 0)
                tiles.update(two_pairs(p, 0, 2))
                for c in range(4):
                    m_load(Pair(p, 0, c), tiles[c])

            def f_store(n, s):
                sp.wait_ge(f_dve[s], F_DVE * (n + 1))
                sp.dma_start(out_rows[:, bass.ds(2 * GB * n + GB * s, GB), :], fx[s]).then_inc(f_saved[s], 16)

            def f_load(n, s):
                after(sp, f_saved[s], 16 * n)
                sp.dma_start(fx[s], x2_rows[:, bass.ds(2 * GB * n + GB * s, GB), :]).then_inc(f_x[s], 16)

            def cycle(i, m, b, f):
                tiles = {}
                for k in range(CY):
                    if m is not None:
                        if k % 2 == 0:
                            tiles.update(two_pairs(m, i, k + 4))
                        m_load(Pair(m, i, k + 4), tiles[k + 4])
                    if b is not None and k in (0, 1):
                        b_load(GU * b + i, k)
                    if f is not None and k in (2, 3) and not (f == 0 and isinstance(i, int)):
                        f_store(GU * f + i - 1, k - 2)
                    if f is not None and k in (4, 5):
                        f_load(GU * f + i, k - 4)
                    if b is not None and k in (4, 5):
                        b_save(GU * b + i, k - 4)

            for s in range(2):
                sp.wait_ge(a_done[s], NG // 4)
            cycles(sp, cycle, None, 0, None)
            for s in range(2):
                sp.wait_ge(b_saved[s], 16 * GU)
            m_first(0)
            for p in range(PARTS):
                cycles(sp, cycle, p, p + 1 if p + 1 < PARTS else None, p - 1 if p else None)
                for s in range(2):
                    sp.wait_ge(b_saved[s], 16 * GU * min(p + 2, PARTS))
                if p + 1 < PARTS:
                    m_first(p + 1)
            cycles(sp, cycle, None, None, PARTS - 1)
            for s in range(2):
                f_store(NG // 2 - 1, s)
            for s in range(2):
                sp.wait_ge(f_saved[s], 16 * (NG // 2))

        @block.gpsimd
        def _(pool):
            st = Steps(pool, const_ready, CONSTS, 0)
            for v, x in ((ident, 0.0), (before, 1.0), (ones, 1.0), (decay_mask, 1.0), (minus_half, -0.5), (e_base, float(np.e)),
                         (scan_keep, 1.0), (cz, 0.0), (e1[0], 0.0), (e1[1], 0.0)):
                st(pool.memset(v, x))
            for v, n, step, base, by in ((iota_l, P + 1, 1, 0, 0), (rev_pos, 1, 0, 1 - P, 1), (part_no, 1, 0, 0, 1), (rev_e, E, -1, E, 0),
                                         (cap_base, E, CAPR, 0, 0)):
                st(pool.iota(v, [[step, n]], base=base, channel_multiplier=by, allow_small_or_imprecise_dtypes=True))
            st.wait()
            st(pool.affine_select(out=ident, in_=ident, compare_op=ALU.not_equal, fill=1.0, base=0,
                                  pattern=[[-1, P]], channel_multiplier=1))
            st(pool.affine_select(out=before, in_=before, compare_op=ALU.is_ge, fill=0.0, base=-1,
                                  pattern=[[1, P]], channel_multiplier=-1))
            st(pool.memset(decay_mask.rearrange("p (b a) -> p b a", a=CH)[:, :, 0:1], 0.0))
            st(pool.memset(scan_keep.rearrange("p (e t) -> p e t", t=GB)[:, :, 0:1], 0.0))
            st(pool.tensor_copy(run, cap_base))
            st.end()

            def rstd(of, sem_, at):
                pool.tensor_tensor(of[2], of[0], minus_half, ALU.pow).then_inc(sem_, 1)
                pool.wait_ge(sem_, at + 1)
                pool.tensor_tensor(of[3], of[1], of[2], ALU.mult).then_inc(sem_, 1)

            def exponents(g, s, sem_):
                pool.tensor_tensor(arg[s], wd[:, bass.ds(PR * g, PR)].unsqueeze(2).broadcast_to([P, PR, P + 1]),
                                   iota_l.unsqueeze(1).broadcast_to([P, PR, P + 1]), ALU.mult).then_inc(sem_, 1)

            pool.wait_ge(table_ready, TABLES)
            with pool.Fori(0, NG // 4) as n:
                for s in range(4):
                    k, kn = s % 2, 2 * n + s // 2
                    pool.wait_ge(k_exp[k], kn)
                    exponents(4 * n + s, k, k_arg[k])
                    pool.wait_ge(a_dve[s], A_DVE * (n + 1))
                    rstd(norm4[s], a_scale[s], 2 * n)

            for s in range(2):
                pool.wait_ge(k_exp[s], NSG // 2)
            with pool.Fori(0, NSG // 2) as n:
                for s in range(2):
                    pool.wait_ge(s_exp[s], 2 * n)
                    pool.tensor_tensor(
                        vrow[s], dt_row[:, bass.ds(2 * SG * n + SG * s, SG)].rearrange("p (q m) -> p q m", m=2).unsqueeze(3).broadcast_to([P, PR, 2, NS]),
                        a_row.unsqueeze(1).unsqueeze(1).broadcast_to([P, PR, 2, NS]), ALU.mult).then_inc(s_arg[s], 1)
                    exponents(2 * n + s, s, s_arg[s])

            def power(of, sem_):
                pool.tensor_tensor(of[2], of[0], minus_half, ALU.pow).then_inc(sem_, 1)

            def send(n, s):
                pool.wait_ge(b_dve[s], B_DVE * n + B_IDX)
                if not isinstance(n, int):
                    apart(pool)
                for k in range(K2):
                    for t in range(GB):
                        pool.indirect_dma_start(list_dram[send.part], bass.IndirectOffsetOnAxis(idx[s][:, k, t:t + 1], 0),
                                                slots[:, 2 + s, t, :], None).then_inc(b_sent[s], 16)

            def gather(n, s):
                after(pool, f_dve[s], F_DVE * n)
                pool.wait_ge(f_idx[s], n + 1)
                if not isinstance(n, int):
                    apart(pool)
                for k in range(K2):
                    for t in range(GB):
                        pool.indirect_dma_start(gat[s][:, k, t, :], None, eo_dram[gather.part],
                                                bass.IndirectOffsetOnAxis(idx_f[s][:, k, t:t + 1], 0)).then_inc(f_got[s], 16)

            def cycle(i, m, b, f):
                if b is not None:
                    nb, send.part = GU * b + i, b
                if f is not None:
                    nf, gather.part = GU * f + i, f
                if b is not None:
                    for s in range(2):
                        pool.wait_ge(b_dve[s], B_DVE * nb + B_VAR1)
                        power(norm4[s], b_scale[s])
                for s in range(2):
                    if f is not None:
                        gather(nf, s)
                    if b is not None and s == 0:
                        for r in range(2):
                            pool.wait_ge(b_dve[r], B_DVE * nb + B_VAR2)
                            power(norm8[r], b_scale[r])
                if b is not None:
                    for s in range(2):
                        pool.wait_ge(b_dve[s], B_DVE * nb + B_GAP)
                        pool.tensor_tensor(eg[s], e_base, gap[s], ALU.pow).then_inc(b_scale[s], 1)
                for s in range(2):
                    if f is not None:
                        pool.wait_ge(f_dve[s], F_DVE * nf + F_VAR)
                        power(norm4[2 + s], f_scale[s])
                    if b is not None:
                        send(nb, s)

            def pad(p):
                pool.wait_ge(q_dve, Q_DVE * p + 2)
                for e in range(E):
                    pool.indirect_dma_start(list_dram[p], bass.IndirectOffsetOnAxis(idx_pad[:, e:e + 1], 0),
                                            zero_row, None).then_inc(q_padded, 16)

            cycles(pool, cycle, None, 0, None)
            pool.memset(zero_row, 0.0).then_inc(tabs_ready, 1)
            pool.iota(tile_no, [[1, MT]], base=0, channel_multiplier=0, allow_small_or_imprecise_dtypes=True).then_inc(tabs_ready, 1)
            pool.iota(steps_k, [[P, TP]], base=0, channel_multiplier=0, allow_small_or_imprecise_dtypes=True).then_inc(tabs_ready, 1)
            pool.wait_ge(tabs_ready, 3)
            pad(0)
            for p in range(PARTS):
                for s in range(2):
                    after(pool, m_out[s], 16 * MU * p)
                if p == 1:
                    pool.wait_ge(q_dve, Q_DVE * 2)
                cycles(pool, cycle, p, p + 1 if p + 1 < PARTS else None, p - 1 if p else None)
                if p + 1 < PARTS:
                    pad(p + 1)
            for s in range(2):
                pool.wait_ge(m_out[s], 16 * MU * PARTS)
            cycles(pool, cycle, None, None, PARTS - 1)

        @block.scalar
        def _(act):
            act.wait_ge(const_in, 16 * 9)
            for v in (a_col, a_row, dt_row):
                last = act.activation(v, v, ACT.Exp)
            last.then_inc(exp_ready, 1)

            act.wait_ge(const_ready, CONSTS)
            for p in range(PARTS):
                with act.Fori(0, GP // 4) as i:
                    n = GP // 4 * p + i
                    for s in range(4):
                        k, kn = s % 2, 2 * n + s // 2
                        act.wait_ge(k_arg[k], kn + 1)
                        act.wait_ge(k_mm[k], kn)
                        act.activation(e2[k], arg[k], ACT.Exp, scale=-1.0).then_inc(k_exp[k], 1)
                        act.wait_ge(a_scale[s], 2 * n + 2)
                        for t in range(GB):
                            last = act.activation(H[:, p, :, bass.ds(4 * GB * i + GB * s + t, 1)].rearrange("p c o -> p (c o)"),
                                                  slots[:, s, t, :], ACT.Identity,
                                                  scale=norm4[s][2][:, t:t + 1], bias=norm4[s][3][:, t:t + 1])
                        last.then_inc(a_done[s], 1)
                    act.wait_ge(w_copied, 2 * n + 2)
                    act.dma_start(w1_dram[:, :, bass.ds(n, 1), :].rearrange("p k o n -> p k (o n)"), wst1).then_inc(w_stored, 16)
                    act.dma_start(w2_dram[:, :, bass.ds(n, 1), :].rearrange("p k o n -> p k (o n)"), wst2).then_inc(w_stored, 16)

            for s in range(2):
                act.wait_ge(k_mm[s], NSG // 2)

            def s_powers(n, s):
                act.wait_ge(s_arg[s], 2 * n + 1)
                act.wait_ge(s_in[s], n)
                act.activation(e1[s].rearrange("p q (h n) -> p q h n", h=3)[:, :, 0:3:2, :], vrow[s], ACT.Exp,
                               scale=rev_pos).then_inc(s_exp[s], 1)
                act.wait_ge(s_arg[s], 2 * n + 2)
                act.wait_ge(s_coef[s], 2 * n)
                act.activation(e2[s], arg[s], ACT.Exp, scale=-1.0).then_inc(s_exp[s], 1)

            def s_copy(n, s):
                act.wait_ge(s_out[s], n + 1)
                for m in range(2):
                    last = act.activation(
                        H[:, :, bass.ds(2 * SG * n + SG * s, SG), :].rearrange("p q (c m) t -> p m c q t", m=2)[:, m],
                        yp[s][:, m].rearrange("p c (q t) -> p c q t", q=PARTS), ACT.Copy)
                last.then_inc(s_copied[s], 1)

            s_powers(0, 0)
            with act.Fori(0, NSG // 2 - 1) as n:
                s_powers(n, 1)
                s_copy(n, 0)
                s_powers(n + 1, 0)
                s_copy(n, 1)
            s_powers(NSG // 2 - 1, 1)
            s_copy(NSG // 2 - 1, 0)
            s_copy(NSG // 2 - 1, 1)
            for s in range(2):
                act.wait_ge(s_copied[s], NSG // 2)

            def b_apply(p, i, s):
                n = GU * p + i
                act.wait_ge(b_dve[s], B_DVE * n + B_BIAS)
                after(act, b_sent[s], SENT * n)
                for t in range(GB):
                    last = act.activation(slots[:, 2 + s, t, :],
                                          H[:, p, :, bass.ds(2 * GB * i + GB * s + t, 1)].rearrange("p c o -> p (c o)"),
                                          ACT.Identity, scale=norm4[s][2][:, t:t + 1], bias=norm4[s][3][:, t:t + 1])
                last.then_inc(b_y[s], 1)

            def b_copy(n, s):
                after(act, b_lt[1 - s], n + s)
                for h in range(2):
                    act.wait_ge(b_tp[s], 2 * n + h + 1)
                    act.activation(tTs[h], tp[h], ACT.Copy).then_inc(b_tT[s], 1)

            def m_xcopy(pair):
                act.wait_ge(m_xp[pair.s], pair.u + 1)
                after(act, m_h[pair.s], pair.u)
                act.activation(xT[pair.s], px, ACT.Copy).then_inc(m_xT[pair.s], 1)

            def m_silu(pair):
                act.wait_ge(m_h[pair.s], pair.u + 1)
                after(act, m_a[pair.s], pair.u)
                act.activation(gate[pair.s], ph[pair.s][:, :, 0:HF], ACT.Silu).then_inc(m_gate[pair.s], 1)

            def m_ocopy(pair):
                act.wait_ge(m_o[pair.s], pair.u + 1)
                after(act, m_out[pair.s], 16 * pair.u)
                act.activation(o_b[pair.s], po, ACT.Copy).then_inc(m_oc[pair.s], 1)
                act.wait_ge(m_oc[pair.s], pair.u + 1)
                eouts = eo_dram[pair.p].rearrange("(j t r) c -> r j t c", t=2, r=P)
                act.dma_start(eouts[:, bass.ds(pair.j, 1)].rearrange("r o t c -> r (o t) c"), o_b[pair.s]).then_inc(m_out[pair.s], 16)

            def f_apply(n, s):
                act.wait_ge(f_dve[s], F_DVE * n + F_BIAS)
                for t in range(GB):
                    last = act.activation(gat[s][:, 1, t, :], gat[s][:, 0, t, :], ACT.Identity,
                                          scale=norm4[2 + s][2][:, t:t + 1], bias=norm4[2 + s][3][:, t:t + 1])
                last.then_inc(f_z[s], 1)

            def cycle(i, m, b, f):
                for k in range(CY):
                    if m is not None:
                        m_silu(Pair(m, i, k + 2))
                        m_xcopy(Pair(m, i, k + 4))
                        m_ocopy(Pair(m, i, k))
                    if f is not None and k == 0 and not (f == 0 and isinstance(i, int)):
                        for s in range(2):
                            f_apply(GU * f + i - 1, s)
                    if b is not None and k == 1:
                        for s in range(2):
                            b_apply(b, i, s)
                    if b is not None and k in (3, 4):
                        b_copy(GU * b + i, k - 3)

            cycles(act, cycle, None, 0, None)
            act.wait_ge(q_dve, Q_DVE)
            for p in range(PARTS):
                pairs = [Pair(p, 0, c) for c in range(MP)]
                if p == 0:
                    m_xcopy(pairs[0])
                    m_xcopy(pairs[1])
                    m_silu(pairs[0])
                m_xcopy(pairs[2])
                m_silu(pairs[1])
                m_xcopy(pairs[3])
                cycles(act, cycle, p, p + 1 if p + 1 < PARTS else None, p - 1 if p else None)
                m_silu(pairs[MP - 2])
                m_ocopy(pairs[MP - 4])
                m_silu(pairs[MP - 1])
                m_ocopy(pairs[MP - 3])
                if p + 1 < PARTS:
                    m_xcopy(Pair(p + 1, 0, 0))
                    m_xcopy(Pair(p + 1, 0, 1))
                    m_silu(Pair(p + 1, 0, 0))
                m_ocopy(pairs[MP - 2])
                m_ocopy(pairs[MP - 1])
            cycles(act, cycle, None, None, PARTS - 1)
            for s in range(2):
                f_apply(NG // 2 - 1, s)

        @block.vector
        def _(dve):
            def moments(st, tiles, s, w, of):
                for t in range(GB):
                    st(dve.bn_stats(stats[w][s][:, t, :], tiles(t)))
                st.wait()
                apart(dve)
                for t in range(GB):
                    st(dve.bn_aggr(mv[w][s][:, t, :], stats[w][s][:, t, :]))
                st.wait()
                st(dve.tensor_scalar(of[0], mv[w][s][:, :, 1], EPS, None, ALU.add))
                st(dve.tensor_scalar(of[1], mv[w][s][:, :, 0], -1.0, None, ALU.mult))

            dve.wait_ge(exp_ready, 1)
            dve.wait_ge(const_ready, CONSTS)
            st = Steps(dve, table_ready, TABLES, 0)
            pairs = dt_row.rearrange("p (q m) -> p q m", m=2)
            for m in range(2):
                rows = slice(NS * m, NS * m + NS)
                st(dve.tensor_scalar(wd[rows, :], pairs[rows, :, m], a_col[rows, :], None, ALU.mult))
            dve.wait_ge(ct_psum, 1)
            st(dve.tensor_copy(ct, ct_p))
            st(dve.tensor_copy(wgT, wg_p))
            st.wait()
            for m in range(2):
                rows = slice(NS * m, NS * m + NS)
                st(dve.tensor_copy(cz[rows, :, m], ct[rows, :]))
            st.end()

            with dve.Fori(0, NG // 4) as n:
                for s in range(4):
                    dve.wait_ge(a_loaded[s], 16 * (n + 1))
                    st = Steps(dve, a_dve[s], A_DVE, n)
                    moments(st, lambda t: slots[:, s, t, :], s % 2, s // 2, norm4[s])
                    st.end()
                dve.wait_ge(w_psum, n + 1)
                dve.wait_ge(w_stored, 32 * n)
                dve.tensor_copy(wst1[:, 0, :], wp1[:, 0, :])
                dve.tensor_copy(wst1[:, 1, :], wp1[:, 1, :]).then_inc(w_copied, 1)
                dve.tensor_copy(wst2, wp2).then_inc(w_copied, 1)

            for s in range(2):
                dve.wait_ge(k_mm[s], NSG // 2)
                dve.wait_ge(a_done[2 + s], NG // 4)
            st = Steps(dve, k_ready, 5, 0)
            dve.tensor_copy(k_rows, kt_p).then_inc(k_row, 1)
            st(dve.memset(k_pad, 0.0))
            st.wait()
            dve.wait_ge(k_tr, 1)
            for h in range(C // P):
                st(dve.tensor_copy(k_pad[:, h, P - 1:2 * P - 1], kr_p[:, h, :]))
            st.wait()
            for h in range(C // P):
                st(dve.tensor_tensor(k_pad[:, h, P - 1:P], k_pad[:, h, P - 1:P], d_col[:, h:h + 1], ALU.add))
            st.end()

            dve.wait_ge(w_stored, 32 * E)
            with dve.Fori(0, NSG // 2) as n:
                for s in range(2):
                    dve.wait_ge(s_exp[s], 2 * n + 2)
                    dve.wait_ge(s_out[s], n)
                    dve.tensor_tensor(e2c[s], e2[s][:, :, 1:P + 1],
                                      ct[:, bass.ds(2 * PR * n + PR * s, PR)].unsqueeze(2).broadcast_to([P, PR, P]),
                                      ALU.mult).then_inc(s_coef[s], 1)
                    dve.tensor_tensor(decay[s].rearrange("p (q t) -> p q t", q=PR), decay_mask.unsqueeze(1).broadcast_to([P, PR, NT]),
                                      e2[s][:, :, P:P + 1].broadcast_to([P, PR, NT]), ALU.mult).then_inc(s_coef[s], 1)
                    dve.wait_ge(s_in[s], n + 1)
                    dve.wait_ge(s_coef[s], 2 * n + 2)
                    dve.tensor_tensor_scan(state[s].rearrange("p q t -> p (q t)"), decay[s], xp[s].rearrange("p q t -> p (q t)"),
                                           0.0, ALU.mult, ALU.add).then_inc(s_state[s], 1)

            def bt(v):
                return v.unsqueeze(2).broadcast_to([P, GB, E])

            def be(v):
                return v.unsqueeze(1).broadcast_to([P, GB, E])

            def bias(st, of):
                st(dve.tensor_tensor(of[3], of[1], of[2], ALU.mult))

            def b_moments(p, i, s):
                st = Steps(dve, b_dve[s], B_DVE, GU * p + i)
                moments(st, lambda t: H[:, p, :, bass.ds(2 * GB * i + GB * s + t, 1)].rearrange("p c o -> p (c o)"), s, 0, norm4[s])
                assert st.done == B_VAR1

            def b_bias(n, s):
                st = Steps(dve, b_dve[s], B_DVE, n, B_VAR1)
                dve.wait_ge(b_scale[s], B_EXP * n + 1)
                st.wait()
                bias(st, norm4[s])
                assert st.done == B_BIAS

            def b_sum(n, s):
                st = Steps(dve, b_dve[s], B_DVE, n, B_BIAS)
                x, rows = slots[:, s], slots[:, 2 + s]
                dve.wait_ge(b_x[s], 16 * (n + 1))
                dve.wait_ge(b_y[s], n + 1)
                st(dve.tensor_tensor(x, x, rows, ALU.add))
                assert st.done == B_SUM
                st.wait()
                moments(st, lambda t: x[:, t, :], s, 1, norm8[s])
                assert st.done == B_VAR2

            def b_rows(n, s):
                st = Steps(dve, b_dve[s], B_DVE, n, B_VAR2)
                x, rows = slots[:, s], slots[:, 2 + s]
                dve.wait_ge(b_scale[s], B_EXP * n + 2)
                st.wait()
                for t in range(GB):
                    st(dve.tensor_scalar(rows[:, t, :], x[:, t, :], norm8[s][1][:, t:t + 1], norm8[s][2][:, t:t + 1], ALU.add, ALU.mult))
                assert st.done == B_ROWS

            def b_choose(n, s):
                st = Steps(dve, b_dve[s], B_DVE, n, B_ROWS)
                dve.wait_ge(b_lt[s], n + 1)
                st(dve.tensor_tensor(lg[s], lp[s], be(bg_row), ALU.add))
                st.wait()
                st(dve.tensor_reduce(best[s], lg[s], AX.X, ALU.max))
                st.wait()
                st(dve.tensor_tensor(tmp[s], lg[s], bt(best[s]), ALU.is_equal))
                st.wait()
                st(dve.tensor_tensor(tmp2[s], tmp[s], be(rev_e), ALU.mult))
                st.wait()
                st(dve.tensor_reduce(pick[s], tmp2[s], AX.X, ALU.max))
                st.wait()
                st(dve.tensor_tensor(oh1[s], be(rev_e), bt(pick[s]), ALU.is_equal))
                st.wait()
                st(dve.scalar_tensor_tensor(lg2[s], oh1[s], -1e30, lg[s], ALU.mult, ALU.add))
                st.wait()
                st(dve.tensor_reduce(best2[s], lg2[s], AX.X, ALU.max))
                st.wait()
                st(dve.tensor_tensor(gap[s], best2[s], best[s], ALU.subtract))
                assert st.done == B_GAP
                st(dve.tensor_tensor(tmp[s], lg2[s], bt(best2[s]), ALU.is_equal))
                st.wait()
                st(dve.tensor_tensor(tmp2[s], tmp[s], be(rev_e), ALU.mult))
                st.wait()
                st(dve.tensor_reduce(pick[s], tmp2[s], AX.X, ALU.max))
                st.wait()
                st(dve.tensor_tensor(oh2[s], be(rev_e), bt(pick[s]), ALU.is_equal))
                st.wait()
                by_tile = chosen[s].rearrange("p (e t) -> p t e", e=E)
                st(dve.tensor_tensor(by_tile, oh1[s], oh2[s], ALU.add))
                st.wait()
                st(dve.tensor_tensor_scan(seen[s], scan_keep, chosen[s], 0.0, ALU.mult, ALU.add))
                assert st.done == B_SEEN

            def b_places(n, s):
                st = Steps(dve, b_dve[s], B_DVE, n, B_SEEN)
                by_tile = chosen[s].rearrange("p (e t) -> p t e", e=E)
                at = 2 * GB * n + GB * s
                st.wait()
                st(dve.tensor_tensor(pos[s], seen[s].rearrange("p (e t) -> p t e", e=E), by_tile, ALU.subtract))
                dve.wait_ge(b_rank, n + 1)
                st(dve.tensor_tensor(rank_base[s], rp[s][:, 0:E], run, ALU.add))
                st.wait()
                st(dve.tensor_tensor(pos[s], pos[s], be(rank_base[s]), ALU.add))
                st(dve.tensor_tensor(run, rp[s][:, E:2 * E], run, ALU.add))
                st.wait()
                st(dve.tensor_tensor(tmp[s], oh1[s], pos[s], ALU.mult))
                st(dve.tensor_tensor(tmp2[s], oh2[s], pos[s], ALU.mult))
                st.wait()
                st(dve.tensor_reduce(slot_tab[:, 0, bass.ds(at, GB)], tmp[s], AX.X, ALU.add))
                st(dve.tensor_reduce(slot_tab[:, 1, bass.ds(at, GB)], tmp2[s], AX.X, ALU.add))
                st.wait()
                after(dve, b_sent[s], SENT * n)
                st(dve.tensor_scalar(idx[s], slot_tab[:, :, bass.ds(at, GB)], 0.0, None, ALU.add))
                assert st.done == B_IDX

            def b_shares(n, s):
                st = Steps(dve, b_dve[s], B_DVE, n, B_IDX)
                at = 2 * GB * n + GB * s
                dve.wait_ge(b_scale[s], B_EXP * n + 3)
                st(dve.tensor_scalar(wsum[s], eg[s], 1.0, None, ALU.add))
                st.wait()
                st(dve.reciprocal(w_tab[:, 0, bass.ds(at, GB)], wsum[s]))
                st.wait()
                st(dve.tensor_tensor(w_tab[:, 1, bass.ds(at, GB)], w_tab[:, 0, bass.ds(at, GB)], eg[s], ALU.mult))
                st.end()
                st.wait()

            def tile_table(p):
                st = Steps(dve, q_dve, Q_DVE, p)
                if p:
                    dve.wait_ge(q_padded, 16 * E * p)
                st(dve.tensor_tensor(counts, run, cap_base, ALU.subtract))
                st(dve.tensor_scalar(idx_pad, run, part_no, None, ALU.add))
                st.wait()
                st(dve.tensor_tensor(over, counts.unsqueeze(2).broadcast_to([P, E, TP]), steps_k.unsqueeze(1).broadcast_to([P, E, TP]), ALU.is_gt))
                st.wait()
                st(dve.tensor_reduce(ntile, over, AX.X, ALU.add))
                st.wait()
                st(dve.tensor_tensor_scan(ends, ones[:, 0:E], ntile, 0.0, ALU.mult, ALU.add))
                st.wait()
                st(dve.tensor_tensor(starts, ends, ntile, ALU.subtract))
                st(dve.tensor_scalar(last_t, ends[:, E - 1:E], -1.0, None, ALU.add))
                st.wait()
                st(dve.tensor_scalar(t_at, tile_no, last_t, None, ALU.min))
                st(dve.scalar_tensor_tensor(delta, starts, float(P), cap_base, ALU.mult, ALU.subtract))
                st.wait()
                st(dve.tensor_tensor(g_e, t_at.unsqueeze(2).broadcast_to([P, MT, E - 1]), ends[:, 0:E - 1].unsqueeze(1).broadcast_to([P, MT, E - 1]), ALU.is_ge))
                st.wait()
                st(dve.tensor_reduce(e_of, g_e, AX.X, ALU.add))
                st.wait()
                st(dve.tensor_tensor(g_e, g_e, ends[:, 0:E - 1].unsqueeze(1).broadcast_to([P, MT, E - 1]), ALU.mult))
                st.wait()
                st(dve.tensor_reduce(st_of, g_e, AX.X, ALU.max))
                st(dve.tensor_tensor(step_d[:, 1:E], delta[:, 1:E], delta[:, 0:E - 1], ALU.subtract))
                st(dve.tensor_copy(run, cap_base))
                st.wait()
                st(dve.tensor_tensor(t_at, t_at, st_of, ALU.subtract))
                st.wait()
                st(dve.scalar_tensor_tensor(in_tile[:, p, :], e_of, float(CAPT), t_at, ALU.mult, ALU.add))
                st(dve.tensor_copy(tile_e[:, p, :], e_of))
                of_part = slot_tab[:, :, TP * p:TP * p + TP]
                steps = g_e.rearrange("p t e -> p (t e)")[:, 0:K2 * TP * (E - 1)].rearrange("p (k t e) -> p k t e", k=K2, e=E - 1)
                for_all = cap_base[:, 1:E].unsqueeze(1).unsqueeze(1).broadcast_to([P, K2, TP, E - 1])
                st(dve.tensor_tensor(steps, of_part.unsqueeze(3).broadcast_to([P, K2, TP, E - 1]), for_all, ALU.is_ge))
                st.wait()
                st(dve.tensor_tensor(steps, steps, step_d[:, 1:E].unsqueeze(1).unsqueeze(1).broadcast_to([P, K2, TP, E - 1]), ALU.mult))
                st.wait()
                st(dve.tensor_reduce(shift, steps, AX.X, ALU.add))
                st.wait()
                st(dve.tensor_tensor(slot_tab_i[:, :, TP * p:TP * p + TP], of_part, shift, ALU.add))
                st.end()
                st.wait()

            def m_mul(pair):
                dve.wait_ge(m_gate[pair.s], pair.u + 1)
                after(dve, m_ap[pair.s], pair.u)
                dve.tensor_tensor(act_b[pair.s], gate[pair.s], ph[pair.s][:, :, HF:DFF], ALU.mult).then_inc(m_a[pair.s], 1)

            def m_acopy(pair):
                dve.wait_ge(m_ap[pair.s], pair.u + 1)
                after(dve, m_o[pair.s], pair.u)
                dve.tensor_copy(aT[pair.s], pa).then_inc(m_aT[pair.s], 1)

            def f_places(n, s):
                after(dve, f_got[s], SENT * n)
                if not isinstance(n, int):
                    apart(dve)
                dve.tensor_copy(idx_f[s], slot_tab_i[:, :, bass.ds(2 * GB * n + GB * s, GB)]).then_inc(f_idx[s], 1)

            def f_sum(n, s):
                st = Steps(dve, f_dve[s], F_DVE, n)
                at = 2 * GB * n + GB * s
                dve.wait_ge(f_got[s], SENT * (n + 1))
                for t in range(GB):
                    st(dve.tensor_scalar(gat[s][:, 0, t, :], gat[s][:, 0, t, :], w_tab[:, 0, bass.ds(at + t, 1)], None, ALU.mult))
                st.wait()
                for t in range(GB):
                    st(dve.scalar_tensor_tensor(gat[s][:, 0, t, :], gat[s][:, 1, t, :], w_tab[:, 1, bass.ds(at + t, 1)],
                                                gat[s][:, 0, t, :], ALU.mult, ALU.add))
                assert st.done == F_SUM

            def f_moments(n, s):
                st = Steps(dve, f_dve[s], F_DVE, n, F_SUM)
                st.wait()
                moments(st, lambda t: gat[s][:, 0, t, :], s, 2, norm4[2 + s])
                assert st.done == F_VAR

            def f_bias(n, s):
                st = Steps(dve, f_dve[s], F_DVE, n, F_VAR)
                dve.wait_ge(f_scale[s], n + 1)
                st.wait()
                bias(st, norm4[2 + s])
                assert st.done == F_BIAS

            def f_add(n, s):
                st = Steps(dve, f_dve[s], F_DVE, n, F_BIAS)
                dve.wait_ge(f_x[s], 16 * (n + 1))
                dve.wait_ge(f_z[s], n + 1)
                st(dve.tensor_tensor(fx[s], fx[s], gat[s][:, 1], ALU.add))
                st.end()

            def cycle(i, m, b, f):
                nb = GU * b + i if b is not None else None
                nf = GU * f + i if f is not None else None
                finish = f is not None and not (f == 0 and isinstance(i, int))
                for k in range(CY):
                    if m is not None:
                        m_acopy(Pair(m, i, k + 1))
                        m_mul(Pair(m, i, k + 2))
                    if b is not None:
                        if k == 0:
                            b_moments(b, i, 0)
                            b_moments(b, i, 1)
                        elif k == 4:
                            b_choose(nb, 0)
                        elif k == 5:
                            b_choose(nb, 1)
                        elif k in (1, 2, 3, 6, 7):
                            for s in range(2):
                                {1: b_bias, 2: b_sum, 3: b_rows, 6: b_places, 7: b_shares}[k](nb, s)
                    if f is not None:
                        if k == 0:
                            for s in range(2):
                                f_places(nf, s)
                                if finish:
                                    f_bias(nf - 1, s)
                        elif k == 1 and finish:
                            for s in range(2):
                                f_add(nf - 1, s)
                        elif k == 4:
                            f_sum(nf, 0)
                        elif k == 5:
                            f_moments(nf, 0)
                        elif k == 6:
                            f_sum(nf, 1)
                        elif k == 7:
                            f_moments(nf, 1)

            for s in range(2):
                dve.wait_ge(s_copied[s], NSG // 2)
            cycles(dve, cycle, None, 0, None)
            dve.wait_ge(tabs_ready, 3)
            tile_table(0)
            for p in range(PARTS):
                pairs = [Pair(p, 0, c) for c in range(MP)]
                if p == 0:
                    m_mul(pairs[0])
                m_acopy(pairs[0])
                m_mul(pairs[1])
                cycles(dve, cycle, p, p + 1 if p + 1 < PARTS else None, p - 1 if p else None)
                m_acopy(pairs[MP - 3])
                m_mul(pairs[MP - 2])
                if p + 1 < PARTS:
                    tile_table(p + 1)
                m_acopy(pairs[MP - 2])
                m_mul(pairs[MP - 1])
                m_acopy(pairs[MP - 1])
                if p + 1 < PARTS:
                    m_mul(Pair(p + 1, 0, 0))
            cycles(dve, cycle, None, None, PARTS - 1)
            for s in range(2):
                f_bias(NG // 2 - 1, s)
            for s in range(2):
                f_add(NG // 2 - 1, s)

        @block.tensor
        def _(pe):
            pe.wait_ge(const_ready, CONSTS)
            pe.wait_ge(const_in, 16 * 9)
            pe.transpose(ct_p, c_rows, ident)
            for k in range(KC):
                last = pe.transpose(wg_p[:, k, :], wg_rows[0:E, P * k:P * k + P], ident[0:E, 0:E])
            last.then_inc(ct_psum, 1)

            pe.wait_ge(table_ready, TABLES)
            with pe.Fori(0, NG // 4) as n:
                for s in range(4):
                    k, kn = s % 2, 2 * n + s // 2
                    pe.wait_ge(k_exp[k], kn + 1)
                    for q in range(PR):
                        last = pe.matmul(kt_p[:, bass.ds(4 * SG * n + SG * s + 2 * q, 2)], e2[k][:, q, 0:P],
                                         cz[:, bass.ds(4 * PR * n + PR * s + q, 1), :].rearrange("p o m -> p (o m)"), start=True, stop=True)
                    last.then_inc(k_mm[k], 1)
                pe.wait_ge(w_loaded, 32 * (n + 1))
                pe.wait_ge(w_copied, 2 * n)
                for k in range(KC):
                    for j in range(DFF // P):
                        pe.transpose(wp1[:, k, P * j:P * j + P], wrow1[:, j, P * k:P * k + P], ident)
                    for j in range(C // P):
                        last = pe.transpose(wp2[:, k, P * j:P * j + P], wrow2[:, j, P * k:P * k + P], ident)
                last.then_inc(w_psum, 1)
            pe.wait_ge(k_row, 1)
            for h in range(C // P):
                last = pe.transpose(kr_p[:, h, :], k_rows[:, P * h:P * h + P], ident)
            last.then_inc(k_tr, 1)

            for s in range(4):
                pe.wait_ge(a_done[s], NG // 4)
            pe.wait_ge(w_copied, 2 * E)

            def channel(m):
                return H[:, :, bass.ds(m, 1), :].rearrange("p q o t -> p q (o t)")

            def s_inputs(n, s):
                pe.wait_ge(s_exp[s], 2 * n + 1)
                pe.wait_ge(s_state[s], n)
                for q in range(PR):
                    for m in range(2):
                        last = pe.matmul(xp[s][:, q, :].rearrange("p (q t) -> p q t", q=PARTS), e1[s][:, q, NS * m:NS * m + P],
                                         channel(2 * SG * n + SG * s + 2 * q + m), start=(m == 0), stop=(m == 1))
                last.then_inc(s_in[s], 1)

            def s_outputs(n, s):
                pe.wait_ge(s_toep[s], 16 * (n + 1))
                pe.wait_ge(s_coef[s], 2 * n + 1)
                pe.wait_ge(s_state[s], n + 1)
                pe.wait_ge(s_copied[s], n)
                for q in range(PR):
                    for m in range(2):
                        y = yp[s][:, m, q, :]
                        rows = slice(NS * m, NS * m + NS)
                        pe.matmul(y.rearrange("p (q t) -> p q t", q=PARTS), toep[s][:, 2 * q + m, :], channel(2 * SG * n + SG * s + 2 * q + m),
                                  start=True, stop=False)
                        last = pe.matmul(y.rearrange("p (b a) -> p b a", a=CH)[:, :, 1:CH], e2c[s][rows, q, :],
                                         state[s][rows, q, :].rearrange("p (b a) -> p b a", a=CH)[:, :, 0:CH - 1], start=False, stop=True)
                last.then_inc(s_out[s], 1)

            s_inputs(0, 0)
            with pe.Fori(0, NSG // 2 - 1) as n:
                s_inputs(n, 1)
                s_outputs(n, 0)
                s_inputs(n + 1, 0)
                s_outputs(n, 1)
            s_inputs(NSG // 2 - 1, 1)
            s_outputs(NSG // 2 - 1, 0)
            s_outputs(NSG // 2 - 1, 1)

            for s in range(2):
                pe.wait_ge(s_copied[s], NSG // 2)

            def b_transpose(n, s, over):
                pe.wait_ge(b_dve[s], B_DVE * n + B_ROWS)
                for h in range(2):
                    if over is None:
                        after(pe, b_tT[1 - s], 2 * (n + s))
                    else:
                        pe.wait_ge((m_xT, m_aT)[h][over[h].s], over[h].u + 1)
                    for t in range(2):
                        for k in range(KC):
                            last = pe.transpose(tp[h][:, t, k, :], slots[:, 2 + s, 2 * h + t, P * k:P * k + P], ident)
                    last.then_inc(b_tp[s], 1)

            def b_logits(n, s):
                if s == 0:
                    after(pe, b_dve[1], B_DVE * n)
                else:
                    pe.wait_ge(b_dve[0], B_DVE * n + B_LG)
                for t in range(GB):
                    if t % 2 == 0:
                        pe.wait_ge(b_tT[s], 2 * n + t // 2 + 1)
                    for k in range(KC):
                        last = pe.matmul(lp[s][:, t, :], tTs[t // 2][:, t % 2, k, :], wgT[:, k, :], start=(k == 0), stop=(k == KC - 1))
                last.then_inc(b_lt[s], 1)

            def b_ranks(n):
                for s in range(2):
                    pe.wait_ge(b_dve[s], B_DVE * n + B_SEEN)
                for s in range(2):
                    for v, w in ((before, 0), (ones, 1)):
                        last = pe.matmul(rp[s][:, E * w:E * w + E], v, seen[s].rearrange("p (e t) -> p e t", e=E)[:, :, GB - 1],
                                         start=True, stop=True)
                last.then_inc(b_rank, 1)

            def two_pairs(p, i, c):
                v = nc.values_load_multi_w_load_instructions(tile_e[0:1, p, bass.ds(2 * CY * i + 2 * c, 4)], engines=(PE,),
                                                             min_val=0, max_val=E - 1)[1]
                return {c: v[0:2], c + 1: v[2:4]}

            def m_xtr(pair):
                pe.wait_ge(m_in[pair.s], 32 * (pair.u + 1))
                after(pe, m_xT[1 - pair.s], pair.u + pair.s)
                for t in range(2):
                    for k in range(KC):
                        last = pe.transpose(px[:, t, k, :], xin[pair.s][:, t, P * k:P * k + P], ident)
                last.then_inc(m_xp[pair.s], 1)

            def m_up(pair, experts):
                pe.wait_ge(m_xT[pair.s], pair.u + 1)
                after(pe, m_a[pair.s], pair.u)
                for t, e in enumerate(experts):
                    for k in range(KC):
                        last = pe.matmul(ph[pair.s][:, t, :], xT[pair.s][:, t, k, :], W1[:, k, bass.ds(e, 1), :].rearrange("p o n -> p (o n)"),
                                         start=(k == 0), stop=(k == KC - 1))
                last.then_inc(m_h[pair.s], 1)

            def m_atr(pair):
                pe.wait_ge(m_a[pair.s], pair.u + 1)
                after(pe, m_aT[1 - pair.s], pair.u + pair.s)
                for t in range(2):
                    for k in range(KC):
                        last = pe.transpose(pa[:, t, k, :], act_b[pair.s][:, t, P * k:P * k + P], ident)
                last.then_inc(m_ap[pair.s], 1)

            def m_down(pair, experts):
                pe.wait_ge(m_aT[pair.s], pair.u + 1)
                after(pe, m_oc[1 - pair.s], pair.u + pair.s)
                for t, e in enumerate(experts):
                    for k in range(KC):
                        last = pe.matmul(po[:, t, :], aT[pair.s][:, t, k, :], W2[:, k, bass.ds(e, 1), :].rearrange("p o n -> p (o n)"),
                                         start=(k == 0), stop=(k == KC - 1))
                last.then_inc(m_o[pair.s], 1)

            def cycle(i, m, b, f):
                nb = GU * b + i if b is not None else None
                of = {}
                for k in range(CY):
                    if m is not None:
                        if k == 0:
                            of.update(two_pairs(m, i, 0))
                        if k % 2 == 0:
                            of.update(two_pairs(m, i, k + 2))
                        m_up(Pair(m, i, k + 2), of[k + 2])
                        if b is not None and k in (4, 5):
                            pe.wait_ge(b_tT[k - 4], 2 * nb + 2)
                        m_atr(Pair(m, i, k + 1))
                    if b is not None and k in (4, 5):
                        b_logits(nb, k - 4)
                    if m is not None:
                        m_xtr(Pair(m, i, k + 4))
                        m_down(Pair(m, i, k), of[k])
                    if b is not None and k in (3, 4):
                        b_transpose(nb, k - 3, None if m is None else (Pair(m, i, k + 4), Pair(m, i, k + 1)))
                    if b is not None and k == 5:
                        b_ranks(nb)

            cycles(pe, cycle, None, 0, None)
            pe.wait_ge(weights_in, 32)
            pe.wait_ge(b_tT[1], 2 * GU)
            for p in range(PARTS):
                pairs = [Pair(p, 0, c) for c in range(MP)]
                if p == 0:
                    pe.wait_ge(q_dve, Q_DVE)
                    m_xtr(pairs[0])
                    m_xtr(pairs[1])
                    m_up(pairs[0], two_pairs(p, 0, 0)[0])
                m_xtr(pairs[2])
                m_up(pairs[1], two_pairs(p, 0, 0)[1])
                m_atr(pairs[0])
                m_xtr(pairs[3])
                cycles(pe, cycle, p, p + 1 if p + 1 < PARTS else None, None)
                of = two_pairs(p, 0, MP - 4)
                of.update(two_pairs(p, 0, MP - 2))
                m_up(pairs[MP - 2], of[MP - 2])
                m_atr(pairs[MP - 3])
                m_down(pairs[MP - 4], of[MP - 4])
                m_up(pairs[MP - 1], of[MP - 1])
                m_atr(pairs[MP - 2])
                m_down(pairs[MP - 3], of[MP - 3])
                m_atr(pairs[MP - 1])
                if p + 1 < PARTS:
                    pe.wait_ge(q_dve, Q_DVE * (p + 2))
                    m_xtr(Pair(p + 1, 0, 0))
                    m_xtr(Pair(p + 1, 0, 1))
                    m_up(Pair(p + 1, 0, 0), two_pairs(p + 1, 0, 0)[0])
                m_down(pairs[MP - 2], of[MP - 2])
                m_down(pairs[MP - 1], of[MP - 1])


_INS = ["L0_attn_u", "L0_attn_A_log", "L0_attn_D", "L0_attn_C_re", "L0_attn_log_dt",
        "L0_ffn_Wg", "L0_ffn_bg", "L0_ffn_w1", "L0_ffn_w2"]
_OUTS = [((B, L, C), "float32")]


def kernel(**inputs):
    import concourse.bacc as _bacc
    from concourse.bass_utils import run_bass_kernel_spmd as _run

    nc = _bacc.Bacc("TRN2", target_bir_lowering=False, num_devices=1)
    arrays, args = {}, []
    for name in _INS:
        a = np.ascontiguousarray(inputs[name])
        arrays[f"in_{name}_dram"] = a
        args.append(nc.dram_tensor(f"in_{name}_dram", a.shape, mybir.dt.from_np(a.dtype), kind="ExternalInput").ap())
    for i, (shape, dtype) in enumerate(_OUTS):
        args.append(nc.dram_tensor(f"out_{i}_dram", shape, mybir.dt.from_np(np.dtype(dtype)), kind="ExternalOutput").ap())
    ssm_moe_block(nc, *args)
    r = _run(nc, [arrays], core_ids=[0])
    return r.results[0]["out_0_dram"]
```

```python
from contextlib import ExitStack

import numpy as np
import concourse.bass as bass
from concourse import mybir

F32 = mybir.dt.float32
I32 = mybir.dt.int32
ALU = mybir.AluOpType
ACT = mybir.ActivationFunctionType
AX = mybir.AxisListType
PE, SP = mybir.EngineType.PE, mybir.EngineType.SP

P = 128
B, L, C = 8, 2048, 256
NS = 64
E, K2 = 8, 2
DFF = 512
HF = DFF // 2
CH = L // P
NT = B * CH
KC = C // P
GB = 4
NG = NT // GB
PARTS = 4
GP = NG // PARTS
TP = NT // PARTS
CAPT = TP + 1
CAPR = CAPT * P
MT = TP * K2 + E
MP = MT // 2
SG = 8
NSG = C // SG
PR = SG // 2
NQ = 16
EPS = 1e-5


class Steps:

    def __init__(self, engine, sem, per, at, done=0):
        self.engine, self.sem, self.per, self.at, self.done = engine, sem, per, at, done

    def __call__(self, instruction):
        instruction.then_inc(self.sem, 1)
        self.done += 1

    def wait(self):
        self.engine.wait_ge(self.sem, self.at * self.per + self.done)

    def end(self):
        assert self.done == self.per, (self.done, self.per)


def ssm_moe_block(nc, u, A_log, D, C_re, log_dt, Wg, bg, w1, w2, out):
    ctx = ExitStack()
    with ctx:
        def sem(name):
            return ctx.enter_context(nc.semaphore(name))

        def sems(name, n=2):
            return [sem(f"{name}{i}") for i in range(n)]

        def region(name, words, dt=F32):
            return ctx.enter_context(nc.sbuf_tensor(name, [P, words], dt))

        class Carve:

            def __init__(self, base, size):
                self.base, self.size, self.at = base, size, 0

            def take(self, *shape):
                n = int(np.prod(shape))
                v = self.base[:, self.at:self.at + n]
                self.at += n
                assert self.at <= self.size, (self.at, self.size)
                names = " ".join(f"d{i}" for i in range(len(shape)))
                if len(shape) == 1:
                    return v
                return v.rearrange(f"p ({names}) -> p {names}", **{f"d{i}": s for i, s in enumerate(shape)})

            def two(self, *shape):
                return [self.take(*shape), self.take(*shape)]

        def scratch(name, shape):
            return nc.dram_tensor(name, shape, F32, kind="Internal").ap()

        toep_dram = scratch("toeplitz", (C, P, P))
        w1_dram = scratch("w1_transposed", (P, KC, E, DFF))
        w2_dram = scratch("w2_transposed", (P, KC, E, C))
        x2_dram = scratch("x_after_ssm", (NT * P, C))
        list_dram = [scratch(f"expert_rows{p}", (E * CAPR, C)) for p in range(PARTS)]
        eo_dram = [scratch(f"expert_out{p}", (MT * P, C)) for p in range(PARTS)]
        u_rows = u.rearrange("b (a p) c -> p (b a) c", p=P)
        x2_rows = x2_dram.rearrange("(t p) c -> p t c", p=P)
        out_rows = out.rearrange("b (a p) c -> p (b a) c", p=P)

        PSZ = C * TP
        hid = region("hid", PARTS * PSZ)
        H = hid[:, :].rearrange("p (q c t) -> p q c t", q=PARTS, c=C)
        wide_size = E * KC * (DFF + C)
        wide = region("wide", wide_size)
        group = region("group", 4 * GB * C)
        slots = group[:, :].rearrange("p (s t c) -> p s t c", s=4, t=GB)
        small = Carve(region("small", 3720), 3720)
        ident = small.take(P)
        before = small.take(P)
        ones = small.take(P)
        minus_half = small.take(GB)
        e_base = small.take(GB)
        part_no = small.take(1)
        rev_e = small.take(E)
        cap_base = small.take(E)
        scan_keep = small.take(E * GB)
        wgT = small.take(KC, E)
        bg_row = small.take(E)
        tTs = small.two(2, KC, P)
        stats = [small.two(GB, 6) for _ in range(3)]
        mv = [small.two(GB, 2) for _ in range(3)]
        norm4 = [[small.take(GB) for _ in range(4)] for _ in range(4)]
        norm8 = [[small.take(GB) for _ in range(4)] for _ in range(2)]
        lg, lg2, tmp, tmp2, oh1, oh2, pos = [small.two(GB, E) for _ in range(7)]
        best, best2, pick, gap, eg, wsum = [small.two(GB) for _ in range(6)]
        chosen, seen = [small.two(E * GB) for _ in range(2)]
        rank_base = small.two(E)
        run = small.take(E)
        w_tab = small.take(K2, NT)
        slot_tab = small.take(K2, NT)
        small_i = Carve(region("small_i", 320, I32), 320)
        slot_tab_i = small_i.take(K2, NT)
        idx = small_i.two(K2, GB)
        idx_f = small_i.two(K2, GB)
        idx_pad = small_i.take(E)
        mb = Carve(hid[:, 0:PSZ], PSZ)
        xin = mb.two(2, C)
        xT = mb.two(2, KC, P)
        gate = mb.two(2, HF)
        act_b = mb.two(2, HF)
        aT = mb.two(2, KC, P)
        o_b = mb.two(2, C)
        tabs_i = Carve(mb.take(2 * PARTS * MT).bitcast(I32), 2 * PARTS * MT)
        in_tile = tabs_i.take(PARTS, MT)
        tile_e = tabs_i.take(PARTS, MT)
        tabs = mb
        over = tabs.take(E, TP)
        zero_row = tabs.take(C)
        tile_no = tabs.take(MT)
        steps_k = tabs.take(TP)
        counts, ntile, ends, starts, delta, step_d = [tabs.take(E) for _ in range(6)]
        last_t = tabs.take(1)
        t_at, e_of, st_of = [tabs.take(MT) for _ in range(3)]
        g_e = tabs.take(MT, E - 1)
        shift = over.rearrange("p e t -> p (e t)")[:, 0:K2 * TP].rearrange("p (k t) -> p k t", k=K2)

        wb = Carve(wide, wide_size)
        toep = wb.two(SG, P)
        vrow = wb.two(PR, 2, NS)
        arg = wb.two(PR, P + 1)
        e1 = wb.two(PR, 3 * NS)
        e2 = wb.two(PR, P + 1)
        wb_e2c = wb.at
        e2c = wb.two(PR, P)
        decay = wb.two(PR * NT)
        wb_state = wb.at
        state = wb.two(PR, NT)
        iota_l = wb.take(P + 1)
        decay_mask = wb.take(NT)
        rev_pos = wb.take(1)
        dt_row = wb.take(C)
        a_row = wb.take(NS)
        a_col = wb.take(1)
        wd = wb.take(C // 2)
        ct = wb.take(C // 2)
        d_col = wb.take(C // P)
        k_rows = wb.take(C)
        k_pad = wb.take(C // P, 2 * P)
        W1v = Carve(wide, wide_size)
        W1 = W1v.take(KC, E, DFF)
        W2 = W1v.take(KC, E, C)
        fb = Carve(hid[:, PSZ:2 * PSZ], PSZ)
        fx = fb.two(GB, C)
        gat = fb.two(K2, GB, C)
        pro = Carve(wide, 2 * SG * P)
        wrow1 = pro.take(DFF // P, C)
        wst1 = pro.take(KC, DFF)
        pro = Carve(wide[:, wb_e2c:], 2 * PR * P)
        wrow2 = pro.take(C // P, C)
        wst2 = pro.take(KC, C)
        pro = Carve(wide[:, wb_state:], 2 * PR * NT)
        cz = pro.take(C // 2, 2)
        c_rows = pro.take(P)
        wg_rows = pro.take(C)

        banks = ctx.enter_context(nc.psum_tensor("banks", [P, 8 * 512], F32))

        def bank(i, n=1):
            return banks[:, 512 * i:512 * (i + n)]

        xp = [bank(i).rearrange("p (q t) -> p q t", q=PR) for i in range(2)]
        yp = [bank(2 + 2 * i, 2).rearrange("p (m q t) -> p m q t", m=2, q=PR) for i in range(2)]
        kt_p = [bank(5 + h)[:, 0:P] for h in range(C // P)]
        ct_p = bank(7)[:, 0:P]
        wg_p = bank(7)[:, P:P + KC * E].rearrange("p (k e) -> p k e", k=KC)
        kr_p = bank(7)[:, 0:C].rearrange("p (h l) -> p h l", h=C // P)
        wp1 = bank(0, 2).rearrange("p (k n) -> p k n", k=KC)
        wp2 = bank(2).rearrange("p (k n) -> p k n", k=KC)
        ph = [bank(2 * i, 2).rearrange("p (t n) -> p t n", t=2) for i in range(2)]
        px = bank(4).rearrange("p (t k n) -> p t k n", t=2, k=KC)
        pa = bank(5).rearrange("p (t k n) -> p t k n", t=2, k=KC)
        po = bank(6).rearrange("p (t n) -> p t n", t=2)
        tp = [px, pa]
        lp = [bank(7)[:, GB * E * i:GB * E * i + GB * E].rearrange("p (t e) -> p t e", t=GB) for i in range(2)]
        rp = [bank(7)[:, 2 * GB * E + 2 * E * i:2 * GB * E + 2 * E * i + 2 * E] for i in range(2)]

        passed = sem("passed")
        const_in, const_ready, exp_ready, table_ready, ct_psum = (
            sem("const_in"), sem("const_ready"), sem("exp_ready"), sem("table_ready"), sem("ct_psum"))
        a_loaded, a_dve, a_scale, a_done = sems("a_loaded", 4), sems("a_dve", 4), sems("a_scale", 4), sems("a_done", 4)
        k_arg, k_exp, k_mm = sems("k_arg"), sems("k_exp"), sems("k_mm")
        k_row, k_tr, k_ready, t_stored = sem("k_row"), sem("k_tr"), sem("k_ready"), sems("t_stored", NQ)
        w_loaded, w_psum, w_copied, w_stored = sem("w_loaded"), sem("w_psum"), sem("w_copied"), sem("w_stored")
        s_toep, s_arg, s_exp, s_coef = sems("s_toep"), sems("s_arg"), sems("s_exp"), sems("s_coef")
        s_in, s_state, s_out, s_copied = sems("s_in"), sems("s_state"), sems("s_out"), sems("s_copied")
        weights_in, tabs_ready = sem("weights_in"), sem("tabs_ready")
        b_x, b_saved, b_pre, b_rstd, b_y = sems("b_x"), sems("b_saved"), sems("b_pre"), sems("b_rstd"), sems("b_y")
        b_dve, b_eg = sems("b_dve"), sems("b_eg")
        b_tp, b_tT, b_lt, b_rank, b_sent = sems("b_tp"), sems("b_tT"), sems("b_lt"), sems("b_rank"), sems("b_sent")
        q_dve, q_padded = sem("q_dve"), sem("q_padded")
        m_in, m_xp, m_xT, m_h, m_gate, m_a = (
            sems("m_in"), sems("m_xp"), sems("m_xT"), sems("m_h"), sems("m_gate"), sems("m_a"))
        m_ap, m_aT, m_o, m_oc, m_out = sems("m_ap"), sems("m_aT"), sems("m_o"), sems("m_oc"), sems("m_out")
        f_x, f_idx, f_got, f_dve, f_scale, f_z, f_saved = (
            sems("f_x"), sems("f_idx"), sems("f_got"), sems("f_dve"), sems("f_scale"), sems("f_z"), sems("f_saved"))

        def apart(engine):
            engine.sem_inc(passed, 1)

        CONSTS = 20
        TABLES = 6
        K_STEPS = 3
        A_DVE = 11
        B_PRE = 25
        B_DVE = 31
        Q_DVE = 22
        F_DVE = 23
        B_VAR1, B_BIAS, B_SUM = 10, 11, 15
        B_ROWS, B_LG, B_GAP, B_SEEN, B_RUN, B_IDX = 4, 5, 13, 19, 23, 28
        Q_ENDS, Q_TILES = 9, 18
        F_SUM, F_VAR = 8, 18
        ROUNDS = NG // 4
        K_ROUNDS = ROUNDS // 2
        K_HALF = K_ROUNDS // 2
        ROUND_Q = 2
        GU = GP // 2
        MU = MP // 2
        SENT = 16 * K2 * GB
        CY = 8
        NCY = GP // 2

        def after(engine, sem_, value):
            if not (isinstance(value, int) and value == 0):
                engine.wait_ge(sem_, value)

        def loop(engine, count, body):
            body(0)
            with engine.Fori(0, count - 1) as i:
                body(i + 1)

        def cycles(engine, cycle, m, b, f):
            first = m == 0 or b == 0 or f == 0
            if first:
                cycle(0, m, b, f, False)
            with engine.Fori(0, NCY - 1 - first) as i:
                cycle(i + 1 if first else i, m, b, f, False)
            cycle(NCY - 1, m, b, f, True)

        def following(i, b, last):
            return (b, i + 1) if not last else (b + 1, 0) if b + 1 < PARTS else None

        class Pair:

            def __init__(self, p, i, c):
                self.p, self.s, self.u, self.j = p, c % 2, MU * p + CY // 2 * i + c // 2, CY * i + c
        block = ctx.enter_context(nc.Block())

        @block.sync
        def _(sp):
            sp.dma_start(a_col[0:NS, :], A_log.rearrange("(n o) -> n o", o=1)).then_inc(const_in, 16)
            sp.dma_start(a_col[NS:2 * NS, :], A_log.rearrange("(n o) -> n o", o=1)).then_inc(const_in, 16)
            sp.dma_start(a_row, A_log.partition_broadcast(P)).then_inc(const_in, 16)
            sp.dma_start(dt_row, log_dt.partition_broadcast(P)).then_inc(const_in, 16)
            sp.dma_start(c_rows, C_re.rearrange("(p m) n -> p (m n)", m=2)).then_inc(const_in, 16)
            for h in range(C // P):
                sp.dma_start(d_col[:, h:h + 1], D[P * h:P * h + P].rearrange("(p o) -> p o", o=1)).then_inc(const_in, 16)
            sp.dma_start(wg_rows[0:E, :], Wg).then_inc(const_in, 16)
            sp.dma_start(bg_row, bg.partition_broadcast(P)).then_inc(const_in, 16)

            def w_load(n):
                after(sp, w_psum, n)
                for v, w in ((wrow1, w1), (wrow2, w2)):
                    sp.dma_start(v, w.rearrange("e (j p) k -> p e j k", p=P)[:, bass.ds(n, 1)].rearrange("p o j k -> p (o j) k")).then_inc(w_loaded, 16)

            def w_store(n):
                sp.wait_ge(w_copied, 2 * n + 2)
                for v, w in ((wst1, w1_dram), (wst2, w2_dram)):
                    sp.dma_start(w[:, :, bass.ds(n, 1), :].rearrange("p k o n -> p k (o n)"), v).then_inc(w_stored, 16)

            def a_round(n, first=False, last=False):
                for s in range(4):
                    after(sp, a_done[s], n)
                    sp.dma_start(slots[:, s], u_rows[:, bass.ds(4 * GB * n + GB * s, GB), :]).then_inc(a_loaded[s], 16)
                if not first:
                    w_store(n - 1)
                if not last:
                    w_load(n + 1)

            w_load(0)
            a_round(0, first=True)
            with sp.Fori(0, ROUNDS - 2) as i:
                a_round(i + 1)
            a_round(ROUNDS - 1, last=True)
            w_store(ROUNDS - 1)

            def b_load(n, s):
                after(sp, b_saved[s], 16 * n)
                if not isinstance(n, int):
                    apart(sp)
                after(sp, b_dve[s], B_DVE * (n - 1) + B_ROWS if not isinstance(n, int) or n else 0)
                sp.dma_start(slots[:, s], u_rows[:, bass.ds(2 * GB * n + GB * s, GB), :]).then_inc(b_x[s], 16)

            def b_save(n, s):
                sp.wait_ge(b_pre[s], B_PRE * n + B_SUM)
                sp.dma_start(x2_rows[:, bass.ds(2 * GB * n + GB * s, GB), :], slots[:, s]).then_inc(b_saved[s], 16)

            sp.wait_ge(w_stored, 32 * E)
            for s in range(2):
                sp.wait_ge(a_done[s], NG // 4)
                b_load(0, s)
            for g in range(NSG):
                sp.wait_ge(t_stored[SG * g * NQ // C], 16)
                if g >= 2:
                    sp.wait_ge(s_out[g % 2], g // 2)
                sp.dma_start(toep[g % 2], toep_dram[SG * g:SG * g + SG].rearrange("c j i -> j c i")).then_inc(s_toep[g % 2], 16)
            for s in range(2):
                sp.wait_ge(s_copied[s], NSG // 2)
            sp.dma_start(W1, w1_dram).then_inc(weights_in, 16)
            sp.dma_start(W2, w2_dram).then_inc(weights_in, 16)
            b_save(0, 0)

            def m_load(pair, tiles):
                after(sp, m_xp[pair.s], pair.u)
                if not isinstance(pair.u, int):
                    apart(sp)
                lists = list_dram[pair.p].rearrange("(n r) c -> n r c", r=P)
                for t, at in enumerate(tiles):
                    sp.dma_start(xin[pair.s][:, t, :], lists[bass.ds(at, 1)].rearrange("o r c -> r (o c)")).then_inc(m_in[pair.s], 16)

            def two_pairs(p, i, c):
                v = nc.values_load_multi_w_load_instructions(in_tile[0:1, p, bass.ds(2 * CY * i + 2 * c, 4)], engines=(SP,),
                                                             min_val=0, max_val=E * CAPT - 1)[1]
                return {c: v[0:2], c + 1: v[2:4]}

            def m_first(p):
                sp.wait_ge(q_dve, Q_DVE * p + 2)
                sp.wait_ge(tabs_ready, 3)
                for e in range(0, E, 4):
                    ends_at = nc.values_load_multi_w_load_instructions(idx_pad[0:1, e:e + 4], engines=(SP,), min_val=0, max_val=E * CAPR - P)[1]
                    for at in ends_at:
                        sp.dma_start(list_dram[p][bass.ds(at, P), :], zero_row).then_inc(q_padded, 16)
                sp.wait_ge(q_dve, Q_DVE * p + Q_TILES)
                tiles = two_pairs(p, 0, 0)
                tiles.update(two_pairs(p, 0, 2))
                sp.wait_ge(q_padded, 16 * E * (p + 1))
                for s in range(2):
                    sp.wait_ge(b_sent[s], SENT * GU * (p + 1))
                for c in range(4):
                    m_load(Pair(p, 0, c), tiles[c])

            def f_store(n, s):
                sp.wait_ge(f_z[s], n + 1)
                sp.dma_start(out_rows[:, bass.ds(2 * GB * n + GB * s, GB), :], fx[s]).then_inc(f_saved[s], 16)

            def f_load(n, s):
                after(sp, f_saved[s], 16 * n)
                if not isinstance(n, int):
                    apart(sp)
                sp.wait_ge(b_saved[s], 16 * (n + 1))
                sp.dma_start(fx[s], x2_rows[:, bass.ds(2 * GB * n + GB * s, GB), :]).then_inc(f_x[s], 16)

            def cycle(i, m, b, f, last):
                tiles = {}
                ahead = b is not None and following(i, b, last) is not None
                if m is None and b is not None:
                    for s in range(2):
                        b_load(GU * b + i + 1, s)
                        b_save(GU * b + i + s, 1 - s)
                    return
                for k in range(CY):
                    if m is not None:
                        if k % 2 == 0:
                            tiles.update(two_pairs(m, i, k + 4))
                        m_load(Pair(m, i, k + 4), tiles[k + 4])
                    if ahead and k == 1:
                        for s in range(2):
                            b_load(GU * b + i + 1, s)
                    if f is not None and k == 2 and not (f == 0 and isinstance(i, int) and i == 0):
                        f_store(GU * f + i - 1, 1)
                    if f is not None and k == 3:
                        for s in range(2):
                            f_load(GU * f + i, s)
                    if ahead and k in (5, 6):
                        b_save(GU * b + i + 1, k - 5)
                    if f is not None and k == 7:
                        f_store(GU * f + i, 0)

            cycles(sp, cycle, None, 0, None)
            b_save(NCY, 1)
            m_first(0)
            for p in range(PARTS):
                cycles(sp, cycle, p, p + 1 if p + 1 < PARTS else None, p - 1 if p else None)
                if p + 1 < PARTS:
                    m_first(p + 1)
            cycles(sp, cycle, None, None, PARTS - 1)
            f_store(NG // 2 - 1, 1)
            for s in range(2):
                sp.wait_ge(f_saved[s], 16 * (NG // 2))

        @block.gpsimd
        def _(pool):
            st = Steps(pool, const_ready, CONSTS, 0)
            for v, x in ((ident, 0.0), (before, 1.0), (ones, 1.0), (decay_mask, 1.0), (minus_half, -0.5), (e_base, float(np.e)),
                         (scan_keep, 1.0), (cz, 0.0), (e1[0], 0.0), (e1[1], 0.0)):
                st(pool.memset(v, x))
            for v, n, step, base, by in ((iota_l, P + 1, 1, 0, 0), (rev_pos, 1, 0, 1 - P, 1), (part_no, 1, 0, 0, 1), (rev_e, E, -1, E, 0),
                                         (cap_base, E, CAPR, 0, 0)):
                st(pool.iota(v, [[step, n]], base=base, channel_multiplier=by, allow_small_or_imprecise_dtypes=True))
            st.wait()
            st(pool.affine_select(out=ident, in_=ident, compare_op=ALU.not_equal, fill=1.0, base=0,
                                  pattern=[[-1, P]], channel_multiplier=1))
            st(pool.affine_select(out=before, in_=before, compare_op=ALU.is_ge, fill=0.0, base=-1,
                                  pattern=[[1, P]], channel_multiplier=-1))
            st(pool.memset(decay_mask.rearrange("p (b a) -> p b a", a=CH)[:, :, 0:1], 0.0))
            st(pool.memset(scan_keep.rearrange("p (e t) -> p e t", t=GB)[:, :, 0:1], 0.0))
            st(pool.tensor_copy(run, cap_base))
            st.end()

            def exponents(g, s, sem_):
                pool.tensor_tensor(arg[s], wd[:, bass.ds(PR * g, PR)].unsqueeze(2).broadcast_to([P, PR, P + 1]),
                                   iota_l.unsqueeze(1).broadcast_to([P, PR, P + 1]), ALU.mult).then_inc(sem_, 1)

            def power(of, sem_):
                pool.tensor_tensor(of[2], of[0], minus_half, ALU.pow).then_inc(sem_, 1)

            def a_round(n, with_k):
                for s in range(4):
                    if with_k:
                        for d in range(2):
                            after(pool, k_exp[d], 4 * n + s)
                            exponents(8 * n + 2 * s + d, d, k_arg[d])
                    pool.wait_ge(a_dve[s], A_DVE * n + A_DVE - 1)
                    power(norm4[s], a_scale[s])

            pool.wait_ge(table_ready, TABLES)
            a_round(0, True)
            with pool.Fori(0, K_ROUNDS - 1) as i:
                a_round(i + 1, True)
            with pool.Fori(0, ROUNDS - K_ROUNDS) as i:
                a_round(i + K_ROUNDS, False)

            for s in range(2):
                pool.wait_ge(k_exp[s], NSG // 2)
            def s_exponents(n):
                for s in range(2):
                    after(pool, s_exp[s], 2 * n)
                    pool.tensor_tensor(
                        vrow[s], dt_row[:, bass.ds(2 * SG * n + SG * s, SG)].rearrange("p (q m) -> p q m", m=2).unsqueeze(3).broadcast_to([P, PR, 2, NS]),
                        a_row.unsqueeze(1).unsqueeze(1).broadcast_to([P, PR, 2, NS]), ALU.mult).then_inc(s_arg[s], 1)
                    exponents(2 * n + s, s, s_arg[s])

            loop(pool, NSG // 2, s_exponents)

            def send(n, s):
                pool.wait_ge(b_dve[s], B_DVE * n + B_IDX)
                if not isinstance(n, int):
                    apart(pool)
                for k in range(K2):
                    for t in range(GB):
                        pool.indirect_dma_start(list_dram[send.part], bass.IndirectOffsetOnAxis(idx[s][:, k, t:t + 1], 0),
                                                slots[:, 2 + s, t, :], None).then_inc(b_sent[s], 16)

            def gather(n, s):
                pool.wait_ge(f_idx[s], n + 1)
                for k in (1, 0):
                    if not (isinstance(n, int) and n == 0):
                        pool.wait_ge(f_dve[s], F_DVE * (n - 1) + (F_SUM if k else F_DVE))
                    if not isinstance(n, int):
                        apart(pool)
                    for t in range(GB):
                        pool.indirect_dma_start(gat[s][:, k, t, :], None, eo_dram[gather.part],
                                                bass.IndirectOffsetOnAxis(idx_f[s][:, k, t:t + 1], 0)).then_inc(f_got[s], 16)

            def make_constants():
                pool.memset(zero_row, 0.0).then_inc(tabs_ready, 1)
                pool.iota(tile_no, [[1, MT]], base=0, channel_multiplier=0, allow_small_or_imprecise_dtypes=True).then_inc(tabs_ready, 1)
                pool.iota(steps_k, [[P, TP]], base=0, channel_multiplier=0, allow_small_or_imprecise_dtypes=True).then_inc(tabs_ready, 1)

            def y_power(n, s):
                pool.wait_ge(b_pre[s], B_PRE * n + B_VAR1)
                power(norm4[s], b_rstd[s])

            def x_power(n, s):
                pool.wait_ge(b_pre[s], B_PRE * n + B_PRE)
                power(norm8[s], b_rstd[s])

            def share_power(n, s):
                pool.wait_ge(b_dve[s], B_DVE * n + B_GAP)
                pool.tensor_tensor(eg[s], e_base, gap[s], ALU.pow).then_inc(b_eg[s], 1)

            def o_power(n, s):
                pool.wait_ge(f_dve[s], F_DVE * n + F_VAR)
                power(norm4[2 + s], f_scale[s])

            def cycle(i, m, b, f, last):
                ahead = b is not None and following(i, b, last) is not None
                if m is None and b is not None:
                    nb, send.part = GU * b + i, b
                    for s in range(2):
                        y_power(nb + 1, s)
                        x_power(nb + s, 1 - s)
                        if s == 0 and last:
                            make_constants()
                        share_power(nb, s)
                        send(nb, s)
                    return
                if m is None:
                    nf, gather.part = GU * f + i, f
                    for s in range(2):
                        o_power(nf, s)
                        if not last:
                            gather(nf + 1, s)
                    return
                if b is not None:
                    nb, send.part = GU * b + i, b
                    for s in range(2):
                        if ahead:
                            y_power(nb + 1, s)
                        share_power(nb, s)
                if f is not None:
                    nf, gather.part = GU * f + i, f
                    o_power(nf, 0)
                if b is not None:
                    for s in range(2):
                        send(nb, s)
                        if ahead:
                            x_power(nb + 1, s)
                if f is not None:
                    o_power(nf, 1)
                    if not last:
                        for s in range(2):
                            gather(nf + 1, s)

            def first_gather(f):
                for s in range(2):
                    pool.wait_ge(m_out[s], 16 * MU * (f + 1))
                gather.part = f
                for s in range(2):
                    gather(GU * f, s)

            for s in range(2):
                y_power(0, s)
            x_power(0, 0)
            cycles(pool, cycle, None, 0, None)
            x_power(NCY, 1)
            for p in range(PARTS):
                if p == 1:
                    pool.wait_ge(q_dve, Q_DVE * 2)
                if p:
                    first_gather(p - 1)
                cycles(pool, cycle, p, p + 1 if p + 1 < PARTS else None, p - 1 if p else None)
            first_gather(PARTS - 1)
            cycles(pool, cycle, None, None, PARTS - 1)

        @block.scalar
        def _(act):
            act.wait_ge(const_in, 16 * 9)
            for v in (a_col, a_row, dt_row):
                last = act.activation(v, v, ACT.Exp)
            last.then_inc(exp_ready, 1)

            act.wait_ge(const_ready, CONSTS)

            def store_blocks(q):
                h, first = divmod(C // NQ * q, P)
                act.wait_ge(k_ready, K_STEPS * (h + 1))
                v = k_pad[first:first + C // NQ, h, P - 1:2 * P - 1]
                skew = bass.AP(v.tensor, v.offset, [v.ap[0], [-1, P], [1, P]])
                act.dma_start(toep_dram[C // NQ * q:C // NQ * q + C // NQ], skew).then_inc(t_stored[q], 16)

            def a_round(p, i, with_k):
                n = GP // 4 * p + i
                for s in range(4):
                    if with_k:
                        for d in range(2):
                            act.wait_ge(k_arg[d], 4 * n + s + 1)
                            after(act, k_mm[d], 4 * n + s)
                            act.activation(e2[d], arg[d], ACT.Exp, scale=-1.0).then_inc(k_exp[d], 1)
                    act.wait_ge(a_dve[s], A_DVE * (n + 1))
                    for t in range(GB):
                        last = act.activation(H[:, p, :, bass.ds(4 * GB * i + GB * s + t, 1)].rearrange("p c o -> p (c o)"),
                                              slots[:, s, t, :], ACT.Identity,
                                              scale=norm4[s][2][:, t:t + 1], bias=norm4[s][3][:, t:t + 1])
                    last.then_inc(a_done[s], 1)
                    if n >= K_HALF and s < ROUND_Q:
                        store_blocks(ROUND_Q * (n - K_HALF) + s)

            for n in range(ROUNDS):
                a_round(n // (GP // 4), n % (GP // 4), n < K_ROUNDS)
            for q in range(ROUND_Q * (ROUNDS - K_HALF), NQ):
                store_blocks(q)

            for s in range(2):
                act.wait_ge(k_mm[s], NSG // 2)

            def s_powers(n, s):
                act.wait_ge(s_arg[s], 2 * n + 1)
                after(act, s_in[s], n)
                act.activation(e1[s].rearrange("p q (h n) -> p q h n", h=3)[:, :, 0:3:2, :], vrow[s], ACT.Exp,
                               scale=rev_pos).then_inc(s_exp[s], 1)
                act.wait_ge(s_arg[s], 2 * n + 2)
                after(act, s_coef[s], 2 * n)
                act.activation(e2[s], arg[s], ACT.Exp, scale=-1.0).then_inc(s_exp[s], 1)

            def s_copy(n, s):
                act.wait_ge(s_out[s], n + 1)
                for m in range(2):
                    last = act.activation(
                        H[:, :, bass.ds(2 * SG * n + SG * s, SG), :].rearrange("p q (c m) t -> p m c q t", m=2)[:, m],
                        yp[s][:, m].rearrange("p c (q t) -> p c q t", q=PARTS), ACT.Copy)
                last.then_inc(s_copied[s], 1)

            s_powers(0, 0)
            s_powers(0, 1)

            def s_step(n):
                for s in range(2):
                    s_powers(n + 1, s)
                    s_copy(n, s)

            loop(act, NSG // 2 - 1, s_step)
            s_copy(NSG // 2 - 1, 0)
            s_copy(NSG // 2 - 1, 1)
            for s in range(2):
                act.wait_ge(s_copied[s], NSG // 2)

            def b_apply(n, s):
                act.wait_ge(b_x[s], 16 * (n + 1))
                act.wait_ge(b_pre[s], B_PRE * n + B_BIAS)
                for t in range(GB):
                    last = act.activation(slots[:, s, t, :], slots[:, s, t, :], ACT.Identity, bias=norm4[s][3][:, t:t + 1])
                last.then_inc(b_y[s], 1)

            def b_copy(n, s):
                after(act, b_lt[1 - s], n + s)
                for h in range(2):
                    act.wait_ge(b_tp[s], 2 * n + h + 1)
                    act.activation(tTs[h], tp[h], ACT.Copy).then_inc(b_tT[s], 1)

            def m_xcopy(pair):
                act.wait_ge(m_xp[pair.s], pair.u + 1)
                after(act, m_h[pair.s], pair.u)
                act.activation(xT[pair.s], px, ACT.Copy).then_inc(m_xT[pair.s], 1)

            def m_silu(pair):
                act.wait_ge(m_h[pair.s], pair.u + 1)
                after(act, m_a[pair.s], pair.u)
                act.activation(gate[pair.s], ph[pair.s][:, :, 0:HF], ACT.Silu).then_inc(m_gate[pair.s], 1)

            def m_ocopy(pair):
                act.wait_ge(m_o[pair.s], pair.u + 1)
                after(act, m_out[pair.s], 16 * pair.u)
                act.activation(o_b[pair.s], po, ACT.Copy).then_inc(m_oc[pair.s], 1)
                act.wait_ge(m_oc[pair.s], pair.u + 1)
                eouts = eo_dram[pair.p].rearrange("(j t r) c -> r j t c", t=2, r=P)
                act.dma_start(eouts[:, bass.ds(pair.j, 1)].rearrange("r o t c -> r (o t) c"), o_b[pair.s]).then_inc(m_out[pair.s], 16)

            def f_apply(n, s):
                act.wait_ge(f_dve[s], F_DVE * (n + 1))
                for t in range(GB):
                    last = act.activation(fx[s][:, t, :], fx[s][:, t, :], ACT.Identity, bias=norm4[2 + s][3][:, t:t + 1])
                last.then_inc(f_z[s], 1)

            def cycle(i, m, b, f, last):
                ahead = b is not None and following(i, b, last) is not None
                if m is None and b is not None:
                    for s in range(2):
                        b_copy(GU * b + i, s)
                        b_apply(GU * b + i + 1, s)
                    return
                for k in range(CY):
                    if m is not None:
                        m_silu(Pair(m, i, k + 2))
                        m_xcopy(Pair(m, i, k + 4))
                        m_ocopy(Pair(m, i, k))
                    if b is not None and k in (0, 1):
                        b_copy(GU * b + i, k)
                    if ahead and k in (2, 3):
                        b_apply(GU * b + i + 1, k - 2)
                    if f is not None and k in (5, 7):
                        f_apply(GU * f + i, (k - 5) // 2)

            for s in range(2):
                b_apply(0, s)
            cycles(act, cycle, None, 0, None)
            act.wait_ge(q_dve, Q_DVE)
            for p in range(PARTS):
                pairs = [Pair(p, 0, c) for c in range(MP)]
                if p == 0:
                    m_xcopy(pairs[0])
                    m_xcopy(pairs[1])
                    m_silu(pairs[0])
                m_xcopy(pairs[2])
                m_silu(pairs[1])
                m_xcopy(pairs[3])
                cycles(act, cycle, p, p + 1 if p + 1 < PARTS else None, p - 1 if p else None)
                m_silu(pairs[MP - 2])
                m_ocopy(pairs[MP - 4])
                m_silu(pairs[MP - 1])
                m_ocopy(pairs[MP - 3])
                if p + 1 < PARTS:
                    m_xcopy(Pair(p + 1, 0, 0))
                    m_xcopy(Pair(p + 1, 0, 1))
                    m_silu(Pair(p + 1, 0, 0))
                m_ocopy(pairs[MP - 2])
                m_ocopy(pairs[MP - 1])
            cycles(act, cycle, None, None, PARTS - 1)

        @block.vector
        def _(dve):
            def moments(st, tiles, s, w, of):
                for t in range(GB):
                    st(dve.bn_stats(stats[w][s][:, t, :], tiles(t)))
                st.wait()
                apart(dve)
                for t in range(GB):
                    st(dve.bn_aggr(mv[w][s][:, t, :], stats[w][s][:, t, :]))
                st.wait()
                st(dve.tensor_scalar(of[0], mv[w][s][:, :, 1], EPS, None, ALU.add))
                st(dve.tensor_scalar(of[1], mv[w][s][:, :, 0], -1.0, None, ALU.mult))

            dve.wait_ge(exp_ready, 1)
            dve.wait_ge(const_ready, CONSTS)
            st = Steps(dve, table_ready, TABLES, 0)
            pairs = dt_row.rearrange("p (q m) -> p q m", m=2)
            for m in range(2):
                rows = slice(NS * m, NS * m + NS)
                st(dve.tensor_scalar(wd[rows, :], pairs[rows, :, m], a_col[rows, :], None, ALU.mult))
            dve.wait_ge(ct_psum, 1)
            st(dve.tensor_copy(ct, ct_p))
            st(dve.tensor_copy(wgT, wg_p))
            st.wait()
            for m in range(2):
                rows = slice(NS * m, NS * m + NS)
                st(dve.tensor_copy(cz[rows, :, m], ct[rows, :]))
            st.end()

            def bias(st, of):
                st(dve.tensor_tensor(of[3], of[1], of[2], ALU.mult))

            def a_round(n):
                def a_moments(s):
                    dve.wait_ge(a_loaded[s], 16 * (n + 1))
                    moments(Steps(dve, a_dve[s], A_DVE, n), lambda t: slots[:, s, t, :], s % 2, s // 2, norm4[s])

                def a_bias(s):
                    st = Steps(dve, a_dve[s], A_DVE, n, A_DVE - 1)
                    dve.wait_ge(a_scale[s], n + 1)
                    st.wait()
                    bias(st, norm4[s])
                    st.end()

                a_moments(0)
                a_moments(1)
                a_bias(0)
                dve.wait_ge(w_psum, n + 1)
                after(dve, w_stored, 32 * n)
                dve.tensor_copy(wst1[:, 0, :], wp1[:, 0, :])
                dve.tensor_copy(wst1[:, 1, :], wp1[:, 1, :]).then_inc(w_copied, 1)
                dve.tensor_copy(wst2, wp2).then_inc(w_copied, 1)
                a_moments(2)
                a_bias(1)
                a_moments(3)
                a_bias(2)
                a_bias(3)

            def k_turn(h):
                for d in range(2):
                    dve.wait_ge(k_mm[d], NSG // 4 * (h + 1))
                st = Steps(dve, k_ready, K_STEPS, h)
                dve.tensor_copy(k_rows[:, P * h:P * h + P], kt_p[h]).then_inc(k_row, 1)
                st(dve.memset(k_pad[:, h, :], 0.0))
                st.wait()
                dve.wait_ge(k_tr, h + 1)
                st(dve.tensor_copy(k_pad[:, h, P - 1:2 * P - 1], kr_p[:, h, :]))
                st.wait()
                st(dve.tensor_tensor(k_pad[:, h, P - 1:P], k_pad[:, h, P - 1:P], d_col[:, h:h + 1], ALU.add))
                st.end()

            for n in range(K_HALF):
                a_round(n)
            k_turn(0)
            for n in range(K_HALF, K_ROUNDS):
                a_round(n)
            k_turn(1)
            with dve.Fori(0, ROUNDS - K_ROUNDS) as i:
                a_round(i + K_ROUNDS)

            dve.wait_ge(w_stored, 32 * E)
            def s_states(n):
                for s in range(2):
                    dve.wait_ge(s_exp[s], 2 * n + 2)
                    after(dve, s_out[s], n)
                    dve.tensor_tensor(e2c[s], e2[s][:, :, 1:P + 1],
                                      ct[:, bass.ds(2 * PR * n + PR * s, PR)].unsqueeze(2).broadcast_to([P, PR, P]),
                                      ALU.mult).then_inc(s_coef[s], 1)
                    dve.tensor_tensor(decay[s].rearrange("p (q t) -> p q t", q=PR), decay_mask.unsqueeze(1).broadcast_to([P, PR, NT]),
                                      e2[s][:, :, P:P + 1].broadcast_to([P, PR, NT]), ALU.mult).then_inc(s_coef[s], 1)
                    dve.wait_ge(s_in[s], n + 1)
                    dve.wait_ge(s_coef[s], 2 * n + 2)
                    dve.tensor_tensor_scan(state[s].rearrange("p q t -> p (q t)"), decay[s], xp[s].rearrange("p q t -> p (q t)"),
                                           0.0, ALU.mult, ALU.add).then_inc(s_state[s], 1)

            loop(dve, NSG // 2, s_states)

            def bt(v):
                return v.unsqueeze(2).broadcast_to([P, GB, E])

            def be(v):
                return v.unsqueeze(1).broadcast_to([P, GB, E])

            def scan_out(p, i, s, t):
                return H[:, p, :, bass.ds(2 * GB * i + GB * s + t, 1)].rearrange("p c o -> p (c o)")

            def b_moments(p, i, s):
                n = GU * p + i
                after(dve, b_y[s], n)
                if not isinstance(n, int):
                    apart(dve)
                st = Steps(dve, b_pre[s], B_PRE, n)
                moments(st, lambda t: scan_out(p, i, s, t), s, 0, norm4[s])
                assert st.done == B_VAR1

            def b_bias(n, s):
                st = Steps(dve, b_pre[s], B_PRE, n, B_VAR1)
                dve.wait_ge(b_rstd[s], 2 * n + 1)
                st.wait()
                bias(st, norm4[s])
                assert st.done == B_BIAS

            def b_sum(p, i, s):
                n = GU * p + i
                st = Steps(dve, b_pre[s], B_PRE, n, B_BIAS)
                x = slots[:, s]
                dve.wait_ge(b_y[s], n + 1)
                if not isinstance(n, int):
                    apart(dve)
                for t in range(GB):
                    st(dve.scalar_tensor_tensor(x[:, t, :], scan_out(p, i, s, t), norm4[s][2][:, t:t + 1], x[:, t, :], ALU.mult, ALU.add))
                assert st.done == B_SUM
                st.wait()
                moments(st, lambda t: x[:, t, :], s, 1, norm8[s])
                st.end()

            def b_rows(n, s):
                st = Steps(dve, b_dve[s], B_DVE, n)
                x, rows = slots[:, s], slots[:, 2 + s]
                after(dve, b_sent[s], SENT * n)
                dve.wait_ge(b_rstd[s], 2 * n + 2)
                dve.wait_ge(b_pre[s], B_PRE * (n + 1))
                for t in range(GB):
                    st(dve.tensor_scalar(rows[:, t, :], x[:, t, :], norm8[s][1][:, t:t + 1], norm8[s][2][:, t:t + 1], ALU.add, ALU.mult))
                assert st.done == B_ROWS

            def b_choose(n, s):
                st = Steps(dve, b_dve[s], B_DVE, n, B_ROWS)
                dve.wait_ge(b_lt[s], n + 1)
                st(dve.tensor_tensor(lg[s], lp[s], be(bg_row), ALU.add))
                st.wait()
                st(dve.tensor_reduce(best[s], lg[s], AX.X, ALU.max))
                st.wait()
                st(dve.tensor_tensor(tmp[s], lg[s], bt(best[s]), ALU.is_equal))
                st.wait()
                st(dve.tensor_tensor(tmp2[s], tmp[s], be(rev_e), ALU.mult))
                st.wait()
                st(dve.tensor_reduce(pick[s], tmp2[s], AX.X, ALU.max))
                st.wait()
                st(dve.tensor_tensor(oh1[s], be(rev_e), bt(pick[s]), ALU.is_equal))
                st.wait()
                st(dve.scalar_tensor_tensor(lg2[s], oh1[s], -1e30, lg[s], ALU.mult, ALU.add))
                st.wait()
                st(dve.tensor_reduce(best2[s], lg2[s], AX.X, ALU.max))
                st.wait()
                st(dve.tensor_tensor(gap[s], best2[s], best[s], ALU.subtract))
                assert st.done == B_GAP
                st(dve.tensor_tensor(tmp[s], lg2[s], bt(best2[s]), ALU.is_equal))
                st.wait()
                st(dve.tensor_tensor(tmp2[s], tmp[s], be(rev_e), ALU.mult))
                st.wait()
                st(dve.tensor_reduce(pick[s], tmp2[s], AX.X, ALU.max))
                st.wait()
                st(dve.tensor_tensor(oh2[s], be(rev_e), bt(pick[s]), ALU.is_equal))
                st.wait()
                by_tile = chosen[s].rearrange("p (e t) -> p t e", e=E)
                st(dve.tensor_tensor(by_tile, oh1[s], oh2[s], ALU.add))
                st.wait()
                st(dve.tensor_tensor_scan(seen[s], scan_keep, chosen[s], 0.0, ALU.mult, ALU.add))
                assert st.done == B_SEEN

            def b_places(n, s):
                st = Steps(dve, b_dve[s], B_DVE, n, B_SEEN)
                by_tile = chosen[s].rearrange("p (e t) -> p t e", e=E)
                at = 2 * GB * n + GB * s
                st.wait()
                st(dve.tensor_tensor(pos[s], seen[s].rearrange("p (e t) -> p t e", e=E), by_tile, ALU.subtract))
                dve.wait_ge(b_rank[s], n + 1)
                st(dve.tensor_tensor(rank_base[s], rp[s][:, 0:E], run, ALU.add))
                st.wait()
                st(dve.tensor_tensor(pos[s], pos[s], be(rank_base[s]), ALU.add))
                st(dve.tensor_tensor(run, rp[s][:, E:2 * E], run, ALU.add))
                assert st.done == B_RUN
                st.wait()
                st(dve.tensor_tensor(tmp[s], oh1[s], pos[s], ALU.mult))
                st(dve.tensor_tensor(tmp2[s], oh2[s], pos[s], ALU.mult))
                st.wait()
                st(dve.tensor_reduce(slot_tab[:, 0, bass.ds(at, GB)], tmp[s], AX.X, ALU.add))
                st(dve.tensor_reduce(slot_tab[:, 1, bass.ds(at, GB)], tmp2[s], AX.X, ALU.add))
                st.wait()
                after(dve, b_sent[s], SENT * n)
                st(dve.tensor_scalar(idx[s], slot_tab[:, :, bass.ds(at, GB)], 0.0, None, ALU.add))
                assert st.done == B_IDX

            def b_shares(n, s):
                st = Steps(dve, b_dve[s], B_DVE, n, B_IDX)
                at = 2 * GB * n + GB * s
                dve.wait_ge(b_eg[s], n + 1)
                st(dve.tensor_scalar(wsum[s], eg[s], 1.0, None, ALU.add))
                st.wait()
                st(dve.reciprocal(w_tab[:, 0, bass.ds(at, GB)], wsum[s]))
                st.wait()
                st(dve.tensor_tensor(w_tab[:, 1, bass.ds(at, GB)], w_tab[:, 0, bass.ds(at, GB)], eg[s], ALU.mult))
                st.end()
                st.wait()

            def list_ends(p):
                st = Steps(dve, q_dve, Q_DVE, p)
                if p:
                    dve.wait_ge(q_padded, 16 * E * p)
                st(dve.tensor_tensor(counts, run, cap_base, ALU.subtract))
                st(dve.tensor_scalar(idx_pad, run, part_no, None, ALU.add))
                st.wait()
                st(dve.tensor_tensor(over, counts.unsqueeze(2).broadcast_to([P, E, TP]), steps_k.unsqueeze(1).broadcast_to([P, E, TP]), ALU.is_gt))
                st.wait()
                st(dve.tensor_reduce(ntile, over, AX.X, ALU.add))
                st.wait()
                st(dve.tensor_tensor_scan(ends, ones[:, 0:E], ntile, 0.0, ALU.mult, ALU.add))
                st.wait()
                st(dve.tensor_tensor(starts, ends, ntile, ALU.subtract))
                st(dve.tensor_scalar(last_t, ends[:, E - 1:E], -1.0, None, ALU.add))
                st.wait()
                st(dve.tensor_scalar(t_at, tile_no, last_t, None, ALU.min))
                st(dve.scalar_tensor_tensor(delta, starts, float(P), cap_base, ALU.mult, ALU.subtract))
                assert st.done == Q_ENDS

            def list_tiles(p):
                st = Steps(dve, q_dve, Q_DVE, p, Q_ENDS)
                st.wait()
                st(dve.tensor_tensor(g_e, t_at.unsqueeze(2).broadcast_to([P, MT, E - 1]), ends[:, 0:E - 1].unsqueeze(1).broadcast_to([P, MT, E - 1]), ALU.is_ge))
                st.wait()
                st(dve.tensor_reduce(e_of, g_e, AX.X, ALU.add))
                st.wait()
                st(dve.tensor_tensor(g_e, g_e, ends[:, 0:E - 1].unsqueeze(1).broadcast_to([P, MT, E - 1]), ALU.mult))
                st.wait()
                st(dve.tensor_reduce(st_of, g_e, AX.X, ALU.max))
                st(dve.tensor_tensor(step_d[:, 1:E], delta[:, 1:E], delta[:, 0:E - 1], ALU.subtract))
                st(dve.tensor_copy(run, cap_base))
                st.wait()
                st(dve.tensor_tensor(t_at, t_at, st_of, ALU.subtract))
                st.wait()
                st(dve.scalar_tensor_tensor(in_tile[:, p, :], e_of, float(CAPT), t_at, ALU.mult, ALU.add))
                st(dve.tensor_copy(tile_e[:, p, :], e_of))
                assert st.done == Q_TILES

            def list_places(p):
                st = Steps(dve, q_dve, Q_DVE, p, Q_TILES)
                st.wait()
                of_part = slot_tab[:, :, TP * p:TP * p + TP]
                steps = g_e.rearrange("p t e -> p (t e)")[:, 0:K2 * TP * (E - 1)].rearrange("p (k t e) -> p k t e", k=K2, e=E - 1)
                for_all = cap_base[:, 1:E].unsqueeze(1).unsqueeze(1).broadcast_to([P, K2, TP, E - 1])
                st(dve.tensor_tensor(steps, of_part.unsqueeze(3).broadcast_to([P, K2, TP, E - 1]), for_all, ALU.is_ge))
                st.wait()
                st(dve.tensor_tensor(steps, steps, step_d[:, 1:E].unsqueeze(1).unsqueeze(1).broadcast_to([P, K2, TP, E - 1]), ALU.mult))
                st.wait()
                st(dve.tensor_reduce(shift, steps, AX.X, ALU.add))
                st.wait()
                st(dve.tensor_tensor(slot_tab_i[:, :, TP * p:TP * p + TP], of_part, shift, ALU.add))
                st.end()
                st.wait()

            def m_mul(pair):
                dve.wait_ge(m_gate[pair.s], pair.u + 1)
                after(dve, m_ap[pair.s], pair.u)
                dve.tensor_tensor(act_b[pair.s], gate[pair.s], ph[pair.s][:, :, HF:DFF], ALU.mult).then_inc(m_a[pair.s], 1)

            def m_acopy(pair):
                dve.wait_ge(m_ap[pair.s], pair.u + 1)
                after(dve, m_o[pair.s], pair.u)
                dve.tensor_copy(aT[pair.s], pa).then_inc(m_aT[pair.s], 1)

            def f_places(n, s):
                after(dve, f_got[s], SENT * n)
                if not isinstance(n, int):
                    apart(dve)
                dve.tensor_copy(idx_f[s], slot_tab_i[:, :, bass.ds(2 * GB * n + GB * s, GB)]).then_inc(f_idx[s], 1)

            def f_sum(n, s):
                st = Steps(dve, f_dve[s], F_DVE, n)
                at = 2 * GB * n + GB * s
                dve.wait_ge(f_got[s], SENT * (n + 1))
                for t in range(GB):
                    st(dve.tensor_scalar(gat[s][:, 0, t, :], gat[s][:, 0, t, :], w_tab[:, 0, bass.ds(at + t, 1)], None, ALU.mult))
                st.wait()
                for t in range(GB):
                    st(dve.scalar_tensor_tensor(gat[s][:, 0, t, :], gat[s][:, 1, t, :], w_tab[:, 1, bass.ds(at + t, 1)],
                                                gat[s][:, 0, t, :], ALU.mult, ALU.add))
                assert st.done == F_SUM

            def f_moments(n, s):
                st = Steps(dve, f_dve[s], F_DVE, n, F_SUM)
                st.wait()
                moments(st, lambda t: gat[s][:, 0, t, :], s, 2, norm4[2 + s])
                assert st.done == F_VAR

            def f_scaled(n, s):
                st = Steps(dve, f_dve[s], F_DVE, n, F_VAR)
                dve.wait_ge(f_scale[s], n + 1)
                dve.wait_ge(f_x[s], 16 * (n + 1))
                st.wait()
                bias(st, norm4[2 + s])
                for t in range(GB):
                    st(dve.scalar_tensor_tensor(fx[s][:, t, :], gat[s][:, 0, t, :], norm4[2 + s][2][:, t:t + 1], fx[s][:, t, :], ALU.mult, ALU.add))
                st.end()

            def cycle(i, m, b, f, last):
                nb = GU * b + i if b is not None else None
                nf = GU * f + i if f is not None else None
                to = following(i, b, last) if b is not None else None
                if m is None and b is not None:
                    for s, other in ((0, (b, i)), (1, to)):
                        b_rows(nb, s)
                        b_moments(*to, s)
                        b_sum(*other, 1 - s)
                        b_choose(nb, s)
                        b_bias(nb + 1, s)
                        b_places(nb, s)
                        b_shares(nb, s)
                    return
                if m is None:
                    for s in range(2):
                        f_sum(nf, s)
                        if not last:
                            f_places(nf + 1, s)
                        f_moments(nf, s)
                        f_scaled(nf, s)
                    return
                for k in range(CY):
                    if b is not None and k == 0:
                        b_rows(nb, 0)
                    if m is not None:
                        m_acopy(Pair(m, i, k + 1))
                        m_mul(Pair(m, i, k + 2))
                    if b is not None:
                        if k == 0:
                            b_rows(nb, 1)
                        elif k in (1, 2):
                            b_choose(nb, k - 1)
                        elif k == 3:
                            b_places(nb, 0)
                            b_places(nb, 1)
                        elif k == 4:
                            b_shares(nb, 0)
                            b_shares(nb, 1)
                    if to:
                        if k in (0, 1):
                            b_moments(*to, k)
                        elif k in (2, 3):
                            b_bias(nb + 1, k - 2)
                        elif k in (4, 5):
                            b_sum(*to, k - 4)
                    if b is not None and last and k in (6, 7):
                        (list_ends if k == 6 else list_tiles)(b)
                    if f is not None:
                        if k == 1:
                            f_sum(nf, 0)
                        elif k == 2:
                            f_moments(nf, 0)
                        elif k == 3:
                            f_scaled(nf, 0)
                        elif k == 5:
                            f_sum(nf, 1)
                            if not last:
                                f_places(nf + 1, 0)
                                f_places(nf + 1, 1)
                        elif k == 6:
                            f_moments(nf, 1)
                        elif k == 7:
                            f_scaled(nf, 1)

            for s in range(2):
                dve.wait_ge(s_copied[s], NSG // 2)
            for s in range(2):
                b_moments(0, 0, s)
                b_bias(0, s)
            b_sum(0, 0, 0)
            cycles(dve, cycle, None, 0, None)
            b_sum(1, 0, 1)
            dve.wait_ge(tabs_ready, 3)
            list_ends(0)
            list_tiles(0)
            list_places(0)
            for p in range(PARTS):
                pairs = [Pair(p, 0, c) for c in range(MP)]
                if p == 0:
                    m_mul(pairs[0])
                m_acopy(pairs[0])
                m_mul(pairs[1])
                if p:
                    for s in range(2):
                        f_places(GU * (p - 1), s)
                cycles(dve, cycle, p, p + 1 if p + 1 < PARTS else None, p - 1 if p else None)
                m_acopy(pairs[MP - 3])
                m_mul(pairs[MP - 2])
                if p + 1 < PARTS:
                    list_places(p + 1)
                m_acopy(pairs[MP - 2])
                m_mul(pairs[MP - 1])
                m_acopy(pairs[MP - 1])
                if p + 1 < PARTS:
                    m_mul(Pair(p + 1, 0, 0))
            for s in range(2):
                f_places(GU * (PARTS - 1), s)
            cycles(dve, cycle, None, None, PARTS - 1)

        @block.tensor
        def _(pe):
            pe.wait_ge(const_ready, CONSTS)
            pe.wait_ge(const_in, 16 * 9)
            pe.transpose(ct_p, c_rows, ident)
            for k in range(KC):
                last = pe.transpose(wg_p[:, k, :], wg_rows[0:E, P * k:P * k + P], ident[0:E, 0:E])
            last.then_inc(ct_psum, 1)

            def w_transpose(n):
                pe.wait_ge(w_loaded, 32 * (n + 1))
                after(pe, w_copied, 2 * n)
                for k in range(KC):
                    for j in range(DFF // P):
                        pe.transpose(wp1[:, k, P * j:P * j + P], wrow1[:, j, P * k:P * k + P], ident)
                    for j in range(C // P):
                        last = pe.transpose(wp2[:, k, P * j:P * j + P], wrow2[:, j, P * k:P * k + P], ident)
                last.then_inc(w_psum, 1)

            def k_sums(n):
                for s in range(4):
                    for d in range(2):
                        g = 8 * n + 2 * s + d
                        h, col = divmod(SG * g, P)
                        pe.wait_ge(k_exp[d], 4 * n + s + 1)
                        for q in range(PR):
                            last = pe.matmul(kt_p[h][:, col + 2 * q:col + 2 * q + 2], e2[d][:, q, 0:P], cz[:, PR * g + q, :], start=True, stop=True)
                        last.then_inc(k_mm[d], 1)

            pe.wait_ge(table_ready, TABLES)
            for n in range(K_ROUNDS):
                w_transpose(n)
                k_sums(n)
                if (n + 1) % K_HALF == 0:
                    h = n // K_HALF
                    pe.wait_ge(k_row, h + 1)
                    pe.transpose(kr_p[:, h, :], k_rows[:, P * h:P * h + P], ident).then_inc(k_tr, 1)
            with pe.Fori(0, ROUNDS - K_ROUNDS) as i:
                w_transpose(i + K_ROUNDS)

            for s in range(4):
                pe.wait_ge(a_done[s], NG // 4)
            pe.wait_ge(w_copied, 2 * E)

            def channel(m):
                return H[:, :, bass.ds(m, 1), :].rearrange("p q o t -> p q (o t)")

            def s_inputs(n, s):
                pe.wait_ge(s_exp[s], 2 * n + 1)
                after(pe, s_state[s], n)
                for q in range(PR):
                    for m in range(2):
                        last = pe.matmul(xp[s][:, q, :].rearrange("p (q t) -> p q t", q=PARTS), e1[s][:, q, NS * m:NS * m + P],
                                         channel(2 * SG * n + SG * s + 2 * q + m), start=(m == 0), stop=(m == 1))
                last.then_inc(s_in[s], 1)

            def s_outputs(n, s):
                pe.wait_ge(s_toep[s], 16 * (n + 1))
                pe.wait_ge(s_coef[s], 2 * n + 1)
                pe.wait_ge(s_state[s], n + 1)
                after(pe, s_copied[s], n)
                for q in range(PR):
                    for m in range(2):
                        y = yp[s][:, m, q, :]
                        rows = slice(NS * m, NS * m + NS)
                        pe.matmul(y.rearrange("p (q t) -> p q t", q=PARTS), toep[s][:, 2 * q + m, :], channel(2 * SG * n + SG * s + 2 * q + m),
                                  start=True, stop=False)
                        last = pe.matmul(y.rearrange("p (b a) -> p b a", a=CH)[:, :, 1:CH], e2c[s][rows, q, :],
                                         state[s][rows, q, :].rearrange("p (b a) -> p b a", a=CH)[:, :, 0:CH - 1], start=False, stop=True)
                last.then_inc(s_out[s], 1)

            s_inputs(0, 0)

            def s_step(n):
                s_inputs(n, 1)
                s_outputs(n, 0)
                s_inputs(n + 1, 0)
                s_outputs(n, 1)

            loop(pe, NSG // 2 - 1, s_step)
            s_inputs(NSG // 2 - 1, 1)
            s_outputs(NSG // 2 - 1, 0)
            s_outputs(NSG // 2 - 1, 1)

            for s in range(2):
                pe.wait_ge(s_copied[s], NSG // 2)

            def b_transpose(n, s, over):
                pe.wait_ge(b_dve[s], B_DVE * n + B_ROWS)
                for h in range(2):
                    if over is None:
                        after(pe, b_tT[1 - s], 2 * (n + s))
                    else:
                        pe.wait_ge((m_xT, m_aT)[h][over[h].s], over[h].u + 1)
                    for t in range(2):
                        for k in range(KC):
                            last = pe.transpose(tp[h][:, t, k, :], slots[:, 2 + s, 2 * h + t, P * k:P * k + P], ident)
                    last.then_inc(b_tp[s], 1)

            def b_logits(n, s, alone):
                if s == 1:
                    pe.wait_ge(b_dve[0], B_DVE * n + (B_RUN if alone else B_LG))
                elif not isinstance(n, int) or n:
                    pe.wait_ge(b_dve[1], B_DVE * (n - 1) + B_RUN)
                for t in range(GB):
                    if t % 2 == 0:
                        pe.wait_ge(b_tT[s], 2 * n + t // 2 + 1)
                    for k in range(KC):
                        last = pe.matmul(lp[s][:, t, :], tTs[t // 2][:, t % 2, k, :], wgT[:, k, :], start=(k == 0), stop=(k == KC - 1))
                last.then_inc(b_lt[s], 1)

            def b_ranks(n, of):
                for s in of:
                    pe.wait_ge(b_dve[s], B_DVE * n + B_SEEN)
                for s in of:
                    for v, w in ((before, 0), (ones, 1)):
                        last = pe.matmul(rp[s][:, E * w:E * w + E], v, seen[s].rearrange("p (e t) -> p e t", e=E)[:, :, GB - 1],
                                         start=True, stop=True)
                    last.then_inc(b_rank[s], 1)

            def two_pairs(p, i, c):
                v = nc.values_load_multi_w_load_instructions(tile_e[0:1, p, bass.ds(2 * CY * i + 2 * c, 4)], engines=(PE,),
                                                             min_val=0, max_val=E - 1)[1]
                return {c: v[0:2], c + 1: v[2:4]}

            def m_xtr(pair):
                pe.wait_ge(m_in[pair.s], 32 * (pair.u + 1))
                after(pe, m_xT[1 - pair.s], pair.u + pair.s)
                for t in range(2):
                    for k in range(KC):
                        last = pe.transpose(px[:, t, k, :], xin[pair.s][:, t, P * k:P * k + P], ident)
                last.then_inc(m_xp[pair.s], 1)

            def m_up(pair, experts):
                pe.wait_ge(m_xT[pair.s], pair.u + 1)
                after(pe, m_a[pair.s], pair.u)
                for t, e in enumerate(experts):
                    for k in range(KC):
                        last = pe.matmul(ph[pair.s][:, t, :], xT[pair.s][:, t, k, :], W1[:, k, bass.ds(e, 1), :].rearrange("p o n -> p (o n)"),
                                         start=(k == 0), stop=(k == KC - 1))
                last.then_inc(m_h[pair.s], 1)

            def m_atr(pair):
                pe.wait_ge(m_a[pair.s], pair.u + 1)
                after(pe, m_aT[1 - pair.s], pair.u + pair.s)
                for t in range(2):
                    for k in range(KC):
                        last = pe.transpose(pa[:, t, k, :], act_b[pair.s][:, t, P * k:P * k + P], ident)
                last.then_inc(m_ap[pair.s], 1)

            def m_down(pair, experts):
                pe.wait_ge(m_aT[pair.s], pair.u + 1)
                after(pe, m_oc[1 - pair.s], pair.u + pair.s)
                for t, e in enumerate(experts):
                    for k in range(KC):
                        last = pe.matmul(po[:, t, :], aT[pair.s][:, t, k, :], W2[:, k, bass.ds(e, 1), :].rearrange("p o n -> p (o n)"),
                                         start=(k == 0), stop=(k == KC - 1))
                last.then_inc(m_o[pair.s], 1)

            def cycle(i, m, b, f, last):
                nb = GU * b + i if b is not None else None
                of = {}
                if m is None:
                    for s in range(2):
                        b_transpose(nb, s, None)
                        b_logits(nb, s, True)
                        b_ranks(nb, (s,))
                    return
                for k in range(CY):
                    if m is not None:
                        if k % 2 == 0:
                            of.update(two_pairs(m, i, k + 2))
                        m_up(Pair(m, i, k + 2), of[k + 2])
                        if b is not None and k in (1, 2):
                            pe.wait_ge(b_tT[k - 1], 2 * nb + 2)
                        m_atr(Pair(m, i, k + 1))
                    if b is not None and k in (1, 2):
                        b_logits(nb, k - 1, False)
                    if b is not None and k == 3:
                        b_ranks(nb, (1, 0))
                    if m is not None:
                        m_xtr(Pair(m, i, k + 4))
                        if k == 0:
                            of.update(two_pairs(m, i, 0))
                        m_down(Pair(m, i, k), of[k])
                    if b is not None and k in (0, 1):
                        b_transpose(nb, k, None if m is None else (Pair(m, i, k + 4), Pair(m, i, k + 1)))

            cycles(pe, cycle, None, 0, None)
            pe.wait_ge(weights_in, 32)
            pe.wait_ge(b_tT[1], 2 * GU)
            for p in range(PARTS):
                pairs = [Pair(p, 0, c) for c in range(MP)]
                if p == 0:
                    pe.wait_ge(q_dve, Q_DVE)
                    m_xtr(pairs[0])
                    m_xtr(pairs[1])
                    m_up(pairs[0], two_pairs(p, 0, 0)[0])
                m_xtr(pairs[2])
                m_up(pairs[1], two_pairs(p, 0, 0)[1])
                m_atr(pairs[0])
                m_xtr(pairs[3])
                cycles(pe, cycle, p, p + 1 if p + 1 < PARTS else None, None)
                of = two_pairs(p, 0, MP - 4)
                of.update(two_pairs(p, 0, MP - 2))
                m_up(pairs[MP - 2], of[MP - 2])
                m_atr(pairs[MP - 3])
                m_down(pairs[MP - 4], of[MP - 4])
                m_up(pairs[MP - 1], of[MP - 1])
                m_atr(pairs[MP - 2])
                m_down(pairs[MP - 3], of[MP - 3])
                m_atr(pairs[MP - 1])
                if p + 1 < PARTS:
                    pe.wait_ge(q_dve, Q_DVE * (p + 1) + Q_TILES)
                    m_xtr(Pair(p + 1, 0, 0))
                    m_xtr(Pair(p + 1, 0, 1))
                    m_up(Pair(p + 1, 0, 0), two_pairs(p + 1, 0, 0)[0])
                m_down(pairs[MP - 2], of[MP - 2])
                m_down(pairs[MP - 1], of[MP - 1])


_INS = ["L0_attn_u", "L0_attn_A_log", "L0_attn_D", "L0_attn_C_re", "L0_attn_log_dt",
        "L0_ffn_Wg", "L0_ffn_bg", "L0_ffn_w1", "L0_ffn_w2"]
_OUTS = [((B, L, C), "float32")]


def kernel(**inputs):
    import concourse.bacc as _bacc
    from concourse.bass_utils import run_bass_kernel_spmd as _run

    nc = _bacc.Bacc("TRN2", target_bir_lowering=False, num_devices=1)
    arrays, args = {}, []
    for name in _INS:
        a = np.ascontiguousarray(inputs[name])
        arrays[f"in_{name}_dram"] = a
        args.append(nc.dram_tensor(f"in_{name}_dram", a.shape, mybir.dt.from_np(a.dtype), kind="ExternalInput").ap())
    for i, (shape, dtype) in enumerate(_OUTS):
        args.append(nc.dram_tensor(f"out_{i}_dram", shape, mybir.dt.from_np(np.dtype(dtype)), kind="ExternalOutput").ap())
    ssm_moe_block(nc, *args)
    r = _run(nc, [arrays], core_ids=[0])
    return r.results[0]["out_0_dram"]
```
